# Optimizing a Trainium2 kernel written in Bass

```python
import numpy as np
import jax
import jax.numpy as jnp

def _softmax(x, axis=-1):
    return jax.nn.softmax(x, axis=axis)

def _gelu(x):
    return jax.nn.gelu(x, approximate=True)

def _silu(x):
    return jax.nn.silu(x)

def _sigmoid(x):
    return jax.nn.sigmoid(x)

def _layernorm(x, axis=-1, eps=1e-05):
    m = jnp.mean(x, axis=axis, keepdims=True)
    v = jnp.var(x, axis=axis, keepdims=True)
    return (x - m) / jnp.sqrt(v + eps)

def _scatter_add(tgt, idx, src, axis=0):
    return tgt.at[idx].add(src)

def _segment_sum(src, seg, n):
    return jax.ops.segment_sum(src, seg, n)
kernel_name = 'mk_xattn_ffn_d1_seqx_r4_3314e6'

def setup_inputs(seed: int=0):
    np.random.seed(seed)
    _w = jnp.asarray

    def _rec_inputs():
        import jax
        import jax.numpy as jnp
        _rk = jax.random.key(seed)
        x = -0.0005207 + 1.001 * jax.random.normal(jax.random.fold_in(_rk, 1), (4, 512, 256), jnp.float32)
        _lenS = 512 - jax.random.randint(jax.random.fold_in(_rk, 7), (4,), 0, max(1, 512 // 4) + 1, jnp.int32)
        _lenS2 = 1024 - jax.random.randint(jax.random.fold_in(_rk, 8), (4,), 0, max(1, 1024 // 4) + 1, jnp.int32)
        _ctx_1024P = jax.random.normal(jax.random.fold_in(_rk, 11), (4, 16, 256), jnp.float32)
        _ctx_1024c = jax.random.dirichlet(jax.random.fold_in(_rk, 511), 0.3 * jnp.ones((16,), jnp.float32), (4, 1024))
        _ctx_1024t = jnp.einsum('bsk,bkd->bsd', _ctx_1024c, _ctx_1024P)
        _ctx_1024t = _ctx_1024t * jax.lax.rsqrt(jnp.mean(jnp.square(_ctx_1024t)) + 1e-12) * 0.953939
        ctx_1024 = -1.52775e-05 + 0.999936 * (_ctx_1024t + 0.3 * jax.random.normal(jax.random.fold_in(_rk, 611), (4, 1024, 256), jnp.float32))
        return (x, ctx_1024)
    x, ctx_1024 = _rec_inputs()

    def _L0_xattn_setup():
        import jax, jax.numpy as jnp
        import numpy as np
        DIM = 256
        HEADS = 16
        DHEAD = 64
        INNER = HEADS * DHEAD
        EPS = 1e-05

        def layer_norm(x, g, b):
            mu = jnp.mean(x, axis=-1, keepdims=True)
            var = jnp.mean(jnp.square(x - mu), axis=-1, keepdims=True)
            return (x - mu) * jax.lax.rsqrt(var + EPS) * g + b

        def apply_rope(x, cos, sin):
            d2 = x.shape[-1] // 2
            x1, x2 = (x[..., :d2], x[..., d2:])
            return jnp.concatenate([x1 * cos - x2 * sin, x2 * cos + x1 * sin], axis=-1)
        key = jax.random.key(seed)
        ks = jax.random.split(key, 10)
        B, N, S = (8, 64, 1024)
        latents = jax.random.normal(ks[0], (B, N, DIM), dtype=jnp.float32)
        context = jax.random.normal(ks[1], (B, S, DIM), dtype=jnp.float32)
        cos = jax.random.uniform(ks[2], (S, DHEAD // 2), dtype=jnp.float32)
        sin = jax.random.uniform(ks[3], (S, DHEAD // 2), dtype=jnp.float32)
        init = lambda k, shp, fan_in: jax.random.normal(k, shp, dtype=jnp.float32) / np.sqrt(fan_in)
        return {'latents': latents, 'context': context, 'cos': cos, 'sin': sin, 'ln_lat_g': jnp.ones((DIM,), jnp.float32), 'ln_lat_b': jnp.zeros((DIM,), jnp.float32), 'ln_ctx_g': jnp.ones((DIM,), jnp.float32), 'ln_ctx_b': jnp.zeros((DIM,), jnp.float32), 'Wq': init(ks[4], (DIM, INNER), DIM), 'Wkv': init(ks[5], (DIM, 2 * INNER), DIM), 'Wo': init(ks[6], (INNER, DIM), INNER), 'bo': jnp.zeros((DIM,), jnp.float32)}
    _L0_xattn_all = _L0_xattn_setup()
    _L0_xattn_in = {k: v for k, v in _L0_xattn_all.items() if k in ('cos', 'sin', 'ln_lat_g', 'ln_lat_b', 'ln_ctx_g', 'ln_ctx_b', 'Wq', 'Wkv', 'Wo', 'bo')}
    del _L0_xattn_all

    def _L0_ffn_setup():
        import jax, jax.numpy as jnp
        import numpy as np
        B, S, D = (4, 1024, 256)
        E, H = (16, 128)
        key = jax.random.key(seed)
        k0, k1, k2, k3 = jax.random.split(key, 4)
        std = 1.0 / np.sqrt(D)
        input_tensor = jax.random.normal(k0, (B, S, D), dtype=jnp.float32)
        expert_sel = jax.random.normal(k1, (E, D), dtype=jnp.float32) * std
        keys = jax.random.normal(k2, (E, D, H), dtype=jnp.float32) * std
        values = jax.random.normal(k3, (E, H, D), dtype=jnp.float32) * (1.0 / np.sqrt(E * H))
        return {'input_tensor': input_tensor, 'expert_sel': expert_sel, 'keys': keys, 'values': values}
    _L0_ffn_all = _L0_ffn_setup()
    _L0_ffn_in = {k: v for k, v in _L0_ffn_all.items() if k in ('expert_sel', 'keys', 'values')}
    del _L0_ffn_all
    return {'x': x, 'ctx_1024': ctx_1024, 'L0_xattn_cos': _L0_xattn_in['cos'], 'L0_xattn_sin': _L0_xattn_in['sin'], 'L0_xattn_ln_lat_g': _L0_xattn_in['ln_lat_g'], 'L0_xattn_ln_lat_b': _L0_xattn_in['ln_lat_b'], 'L0_xattn_ln_ctx_g': _L0_xattn_in['ln_ctx_g'], 'L0_xattn_ln_ctx_b': _L0_xattn_in['ln_ctx_b'], 'L0_xattn_Wq': _L0_xattn_in['Wq'], 'L0_xattn_Wkv': _L0_xattn_in['Wkv'], 'L0_xattn_Wo': _L0_xattn_in['Wo'], 'L0_xattn_bo': _L0_xattn_in['bo'], 'L0_ffn_expert_sel': _L0_ffn_in['expert_sel'], 'L0_ffn_keys': _L0_ffn_in['keys'], 'L0_ffn_values': _L0_ffn_in['values']}

def reference(x, ctx_1024, L0_xattn_cos, L0_xattn_sin, L0_xattn_ln_lat_g, L0_xattn_ln_lat_b, L0_xattn_ln_ctx_g, L0_xattn_ln_ctx_b, L0_xattn_Wq, L0_xattn_Wkv, L0_xattn_Wo, L0_xattn_bo, L0_ffn_expert_sel, L0_ffn_keys, L0_ffn_values):
    import jax
    import jax.numpy as jnp

    def _L0_xattn_ref(latents, context, cos, sin, ln_lat_g, ln_lat_b, ln_ctx_g, ln_ctx_b, Wq, Wkv, Wo, bo):
        import jax, jax.numpy as jnp
        import numpy as np
        DIM = 256
        HEADS = 16
        DHEAD = 64
        INNER = HEADS * DHEAD
        EPS = 1e-05

        def layer_norm(x, g, b):
            mu = jnp.mean(x, axis=-1, keepdims=True)
            var = jnp.mean(jnp.square(x - mu), axis=-1, keepdims=True)
            return (x - mu) * jax.lax.rsqrt(var + EPS) * g + b

        def apply_rope(x, cos, sin):
            d2 = x.shape[-1] // 2
            x1, x2 = (x[..., :d2], x[..., d2:])
            return jnp.concatenate([x1 * cos - x2 * sin, x2 * cos + x1 * sin], axis=-1)
        b, n, _ = latents.shape
        s = context.shape[1]
        lat = layer_norm(latents, ln_lat_g, ln_lat_b)
        ctx = layer_norm(context, ln_ctx_g, ln_ctx_b)
        q = (lat @ Wq).reshape(b, n, HEADS, DHEAD).transpose(0, 2, 1, 3)
        kv = ctx @ Wkv
        k, v = jnp.split(kv, 2, axis=-1)
        k = k.reshape(b, s, HEADS, DHEAD).transpose(0, 2, 1, 3)
        v = v.reshape(b, s, HEADS, DHEAD).transpose(0, 2, 1, 3)
        k = apply_rope(k, cos[None, None], sin[None, None])
        scale = DHEAD ** (-0.5)
        attn = jnp.einsum('bhnd,bhsd->bhns', q, k) * scale
        attn = jnp.clip(attn, -11.0, 11.0)
        attn = jax.nn.softmax(attn, axis=-1)
        out = jnp.einsum('bhns,bhsd->bhnd', attn, v)
        out = out.transpose(0, 2, 1, 3).reshape(b, n, INNER)
        return out @ Wo + bo

    def _L0_ffn_ref(input_tensor, expert_sel, keys, values):
        import jax, jax.numpy as jnp
        import numpy as np
        B, S, D = (4, 1024, 256)
        E, H = (16, 128)
        sel = jax.nn.sigmoid(jnp.einsum('bsd,ed->bse', input_tensor, expert_sel))
        scores = jax.nn.relu(jnp.einsum('bsd,edh->bseh', input_tensor, keys))
        out = jnp.einsum('bseh,ehv,bse->bsv', scores, values, sel)
        return out
    x = x + _L0_xattn_ref(_layernorm(x, axis=-1), ctx_1024, L0_xattn_cos, L0_xattn_sin, L0_xattn_ln_lat_g, L0_xattn_ln_lat_b, L0_xattn_ln_ctx_g, L0_xattn_ln_ctx_b, L0_xattn_Wq, L0_xattn_Wkv, L0_xattn_Wo, L0_xattn_bo)
    x = x + _L0_ffn_ref(_layernorm(x, axis=-1), L0_ffn_expert_sel, L0_ffn_keys, L0_ffn_values)
    return x

_drawn_inputs = setup_inputs


def setup_inputs(seed=0):
    import zlib

    import numpy as np

    out = dict(_drawn_inputs(seed))
    spreads = {'L0_xattn_ln_lat_g': (1.0, 0.6),
     'L0_xattn_ln_lat_b': (0.0, 0.648),
     'L0_xattn_ln_ctx_g': (1.0, 0.2),
     'L0_xattn_ln_ctx_b': (0.0, 0.1),
     'L0_xattn_bo': (0.0, 0.1)}
    factors = {'L0_xattn_cos': 5.676, 'L0_xattn_sin': 5.661}
    for name, (base, spread) in spreads.items():
        noise = np.random.default_rng([zlib.crc32(name.encode()), seed]).standard_normal(out[name].shape)
        drawn = base * np.exp(spread * noise) if base else spread * noise
        out[name] = jnp.asarray(drawn.astype(out[name].dtype))
    for name, factor in factors.items():
        out[name] = (out[name] * factor).astype(out[name].dtype)
    return out
```

```python
from contextlib import ExitStack

import concourse.bass as bass
from concourse import mybir

F32 = mybir.dt.float32
F32R = mybir.dt.float32r
ALU = mybir.AluOpType
ACT = mybir.ActivationFunctionType

P = 128
DMA = 16
B, NQ, D = 4, 512, 256
S = 1024
HEADS, DH = 16, 64
INNER = HEADS * DH
KT = D // P
PAIRS = HEADS // 2
NPAIR = B * PAIRS
STEPS = 8
ALL = B * NQ
EXPERTS, HID = 16, 128
CHUNKS = ALL // 512
EPS = 1e-5
CLIP_HI = 59874.141715197816
CLIP_LO = 1.670170079024566e-05
FIRST_TILES = 9
LAG = 2
RING = 4


def wait(eng, sem, value):
    if isinstance(value, int) and value <= 0:
        return
    eng.wait_ge(sem, value)


def raw(t):
    return t[:].bitcast(F32)


def attention_phase(nc, x, ctx_in, cosT, sinT, cols, Wq, Wkv, Wo, yT):
    with ExitStack() as st:
        def sb(name, shape, dt=F32):
            return st.enter_context(nc.sbuf_tensor(name, shape, dt))

        def psum(name, shape):
            return st.enter_context(nc.psum_tensor(name, shape, F32))

        def sem(name):
            return st.enter_context(nc.semaphore(name))

        ident = sb("ident", [P, P])
        cos_sb = sb("cos_sb", [P, S])
        sin_sb = sb("sin_sb", [P, S])
        col_sb = sb("col_sb", [P, 10])
        ctx_raw = [sb(f"ctx_raw{i}", [P, D]) for i in range(2)]
        x_raw = [sb(f"x_raw{i}", [64, D]) for i in range(2)]
        bn_c = sb("bn_c", [P, 6])
        bn_x = sb("bn_x", [64, 6])
        mv_c = sb("mv_c", [P, 2])
        mv_x = sb("mv_x", [64, 2])
        rstd_c = sb("rstd_c", [P, 2])
        rx = sb("rx", [64, 7])
        power = sb("power", [P, 1])
        eps = sb("eps", [P, 1])
        carry_pool = sb("carry_pool", [P, 1])
        carry_dve = sb("carry_dve", [P, 1])
        ctx_n = sb("ctx_n", [P, D])
        x_n = sb("x_n", [64, D])
        ctx_t32 = sb("ctx_t32", [P, KT, P])
        x_t32 = sb("x_t32", [P, KT, 64])
        ctxT_hi = sb("ctxT_hi", [P, 2, KT, S], F32R)
        ctxT_lo = sb("ctxT_lo", [P, 2, KT, S], F32R)
        xT_hi = sb("xT_hi", [P, 2, KT, NQ], F32R)
        xT_lo = sb("xT_lo", [P, 2, KT, NQ], F32R)
        WC = 3 * KT * P + D
        w_raw = sb("w_raw", [P, WC])
        w_hi = [sb(f"w_hi{i}", [P, WC], F32R) for i in range(2)]
        w_lo = [sb(f"w_lo{i}", [P, WC], F32R) for i in range(2)]
        k32 = sb("k32", [P, S])
        k_swap = sb("k_swap", [P, S])
        k_hi = sb("k_hi", [P, S], F32R)
        k_lo = sb("k_lo", [P, S], F32R)
        k_stack = [[sb(f"k_stack{i}{h}", [P, S], F32R) for h in range(2)] for i in range(2)]
        q_hi = sb("q_hi", [P, NQ], F32R)
        q_lo = sb("q_lo", [P, NQ], F32R)
        q_hh = [[sb(f"q_hh{i}{h}", [P, NQ], F32R) for h in range(2)] for i in range(2)]
        q_ll = [[sb(f"q_ll{i}{h}", [P, NQ], F32R) for h in range(2)] for i in range(2)]
        vT32 = sb("vT32", [P, S])
        v_aug = [sb(f"v_aug{i}", [P, S // P, 3 * DH]) for i in range(2)]
        probs = [sb(f"probs{i}", [P, 2, NQ]) for i in range(RING)]
        o_raw = sb("o_raw", [P, NQ])
        den = sb("den", [P, NQ])
        o_hi = sb("o_hi", [P, NQ], F32R)
        o_lo = sb("o_lo", [P, NQ], F32R)

        score_ps = [psum(f"score_ps{i}", [P, 2, NQ]) for i in range(2)]
        o_ps = [psum(f"o_ps{h}", [P, NQ]) for h in range(2)]
        job_ps = [psum(f"job_ps{i}", [P, 512]) for i in range(2)]

        consts_loaded = sem("consts_loaded")
        ident_zero = sem("ident_zero")
        ident_ready = sem("ident_ready")
        sin_signed = sem("sin_signed")
        y_zeroed = sem("y_zeroed")
        y_biased = sem("y_biased")
        ones_ready = sem("ones_ready")
        tile_loaded = [sem(f"tile_loaded{i}") for i in range(2)]
        bn_done = sem("bn_done")
        stats_ready = sem("stats_ready")
        rstd_step = sem("rstd_step")
        power_ready = sem("power_ready")
        rstd_ready = sem("rstd_ready")
        normed = sem("normed")
        turned = sem("turned")
        affine_done = sem("affine_done")
        tile_hi = sem("tile_hi")
        tile_split = sem("tile_split")
        w_loaded = sem("w_loaded")
        w_hi_done = sem("w_hi_done")
        w_split = sem("w_split")
        k_projected = sem("k_projected")
        k_evac = sem("k_evac")
        k_swapped = sem("k_swapped")
        k_times = sem("k_times")
        k_roped = sem("k_roped")
        k_hi_done = sem("k_hi_done")
        k_split = sem("k_split")
        k_stacked = sem("k_stacked")
        q_projected = sem("q_projected")
        q_hi_done = sem("q_hi_done")
        q_split = sem("q_split")
        q_stacked = sem("q_stacked")
        v_projected = sem("v_projected")
        v_evac = sem("v_evac")
        v_turned = sem("v_turned")
        v_ready = sem("v_ready")
        scores_ready = sem("scores_ready")
        exp_done = sem("exp_done")
        clipped = sem("clipped")
        pv_done = sem("pv_done")
        o_evac = [sem("o_evac_a"), sem("o_evac_b")]
        den_inv = sem("den_inv")
        o_scaled = sem("o_scaled")
        o_hi_done = sem("o_hi_done")
        o_split = sem("o_split")
        y_projected = sem("y_projected")
        y_added = sem("y_added")

        g_lat, b_lat, g_ctx, b_ctx, bo = (col_sb[:, 2 * i:2 * i + 2] for i in range(5))

        def w_part(w, which, k):
            at = (which * KT + k) * P
            return w[:, at:at + P]

        block = st.enter_context(nc.Block())

        @block.sync
        def _(sp):
            def load_tile(t):
                wait(sp, normed, 2 * (t - 1))
                slot = t % 2 if isinstance(t, int) else t_slot[0]
                tt = t % (B * STEPS)
                sp.dma_start(ctx_raw[slot][:], ctx_in[bass.ds(tt * P, P), :]).then_inc(tile_loaded[slot], DMA)
                sp.dma_start(x_raw[slot][:], x[bass.ds(tt * 64, 64), :]).then_inc(tile_loaded[slot], DMA)

            t_slot = [0]

            def load_weights(w, has_wo=True):
                wait(sp, w_split, w)
                p = w % PAIRS
                for which, src, off in ((0, Wq, 0), (1, Wkv, 0), (2, Wkv, INNER)):
                    at = which * KT * P
                    sp.dma_start(
                        w_raw[:, at:at + KT * P].rearrange("c (k n) -> c k n", k=KT),
                        src[:, bass.ds(p * P + off, P)].rearrange("(k c) n -> c k n", k=KT),
                    ).then_inc(w_loaded, DMA)
                pw = (w + PAIRS - 2) % PAIRS
                sp.dma_start(w_raw[:, 3 * KT * P:], Wo[bass.ds(pw * P, P), :]).then_inc(w_loaded, DMA)

            def swap_k(p):
                wait(sp, k_evac, 2 * p + 2)
                wait(sp, k_roped, p)
                for q in range(4):
                    a, b = 32 * q, 32 * (q ^ 1)
                    sp.dma_start(k_swap[a:a + 32, :], k32[b:b + 32, :]).then_inc(k_swapped, DMA)

            def stack_q(p, par):
                wait(sp, q_split, p + 1)
                for h in range(2):
                    src = slice(DH * h, DH * h + DH)
                    for half in range(2):
                        dst = slice(DH * half, DH * half + DH)
                        sp.dma_start(raw(q_hh[par][h])[dst, :], raw(q_hi)[src, :]).then_inc(q_stacked, DMA)
                        sp.dma_start(raw(q_ll[par][h])[dst, :], raw(q_lo)[src, :]).then_inc(q_stacked, DMA)

            def stack_k(p, par):
                wait(sp, k_split, p + 1)
                for h in range(2):
                    src = slice(DH * h, DH * h + DH)
                    sp.dma_start(raw(k_stack[par][h])[0:DH, :], raw(k_hi)[src, :]).then_inc(k_stacked, DMA)
                    sp.dma_start(raw(k_stack[par][h])[DH:P, :], raw(k_lo)[src, :]).then_inc(k_stacked, DMA)

            load_tile(0)
            load_weights(0)
            for q in range(4):
                rows = slice(32 * q, 32 * q + 32)
                sp.dma_start(cos_sb[rows, :], cosT).then_inc(consts_loaded, DMA)
                sp.dma_start(sin_sb[rows, :], sinT).then_inc(consts_loaded, DMA)
            sp.dma_start(col_sb[:], cols).then_inc(consts_loaded, DMA)
            load_tile(1)
            load_weights(1)
            for t in range(2, FIRST_TILES + 1):
                load_tile(t)
            load_weights(2)
            swap_k(0)
            stack_q(0, 0)
            stack_k(0, 0)

            def iteration(n, par, project, prep):
                if project:
                    swap_k(n + 1)
                if prep:
                    t_slot[0] = par
                    load_tile(n + FIRST_TILES + 1)
                if project:
                    stack_q(n + 1, 1 - par)
                    load_weights(n + 3)
                    stack_k(n + 1, 1 - par)

            iteration(0, 0, True, True)
            iteration(1, 1, True, True)
            with sp.Fori(1, NPAIR // 2 - 1) as m:
                iteration(2 * m, 0, True, True)
                iteration(2 * m + 1, 1, True, True)
            iteration(NPAIR - 2, 0, True, False)

        @block.gpsimd
        def _(pool):
            pool.memset(ident[:], 0.0).then_inc(ident_zero, 1)
            pool.wait_ge(ident_zero, 1)
            pool.affine_select(out=ident[:], in_=ident[:], compare_op=ALU.not_equal, fill=1.0, base=0,
                               pattern=[[-1, P]], channel_multiplier=1).then_inc(ident_ready, 1)

            def rstd(t):
                wait(pool, stats_ready, 2 * t + 2)
                wait(pool, normed, 2 * t)
                pool.tensor_tensor(rstd_c[:, 0:1], mv_c[:, 1:2], eps[:], ALU.add).then_inc(rstd_step, 1)
                pool.tensor_tensor(rx[:, 0:1], mv_x[:, 1:2], eps[0:64, :], ALU.add).then_inc(rstd_step, 1)
                pool.wait_ge(rstd_step, 7 * t + 1)
                pool.tensor_tensor(rstd_c[:, 1:2], rstd_c[:, 0:1], power[:], ALU.pow).then_inc(rstd_ready, 1)
                pool.wait_ge(rstd_step, 7 * t + 2)
                pool.tensor_tensor(rx[:, 1:2], rx[:, 0:1], power[0:64, :], ALU.pow).then_inc(rstd_step, 1)
                pool.wait_ge(rstd_step, 7 * t + 3)
                pool.tensor_tensor(rx[:, 2:3], rx[:, 1:2], rx[:, 1:2], ALU.mult).then_inc(rstd_step, 1)
                pool.wait_ge(rstd_step, 7 * t + 4)
                pool.tensor_tensor(rx[:, 3:4], rx[:, 2:3], mv_x[:, 1:2], ALU.mult).then_inc(rstd_step, 1)
                pool.wait_ge(rstd_step, 7 * t + 5)
                pool.tensor_tensor(rx[:, 4:5], rx[:, 3:4], eps[0:64, :], ALU.add).then_inc(rstd_step, 1)
                pool.wait_ge(rstd_step, 7 * t + 6)
                pool.tensor_tensor(rx[:, 5:6], rx[:, 4:5], power[0:64, :], ALU.pow).then_inc(rstd_step, 1)
                pool.wait_ge(rstd_step, 7 * t + 7)
                pool.tensor_tensor(rx[:, 6:7], rx[:, 5:6], rx[:, 1:2], ALU.mult).then_inc(rstd_ready, 1)

            def split_tile(t):
                wait(pool, affine_done, 4 * t + 4)
                bp = (t // STEPS) % 2
                cs = t % STEPS
                c_hi = ctxT_hi[:, bass.ds(bp, 1), :, bass.ds(cs * P, P)]
                c_lo = ctxT_lo[:, bass.ds(bp, 1), :, bass.ds(cs * P, P)]
                x_hi = xT_hi[:, bass.ds(bp, 1), :, bass.ds(cs * 64, 64)]
                x_lo = xT_lo[:, bass.ds(bp, 1), :, bass.ds(cs * 64, 64)]
                c32 = ctx_t32[:, :, :].rearrange("p (a k) n -> p a k n", a=1)
                x32 = x_t32[:, :, :].rearrange("p (a k) n -> p a k n", a=1)
                pool.tensor_copy(c_hi, c32).then_inc(tile_hi, 1)
                pool.tensor_copy(x_hi, x32).then_inc(tile_hi, 1)
                pool.wait_ge(tile_hi, 2 * t + 2)
                pool.tensor_tensor(c_lo, c32, c_hi, ALU.subtract).then_inc(tile_split, 1)
                pool.tensor_tensor(x_lo, x32, x_hi, ALU.subtract).then_inc(tile_split, 1)

            def split_weights(w, par):
                wait(pool, w_loaded, 4 * DMA * (w + 1))
                wait(pool, v_projected, 2 * (w - 1))
                wait(pool, y_projected, 2 * (w - 3))
                pool.tensor_tensor(carry_pool[:], eps[:], power[:], ALU.add)
                pool.tensor_copy(w_hi[par][:], w_raw[:]).then_inc(w_hi_done, 1)
                pool.wait_ge(w_hi_done, w + 1)
                pool.tensor_tensor(w_lo[par][:], w_raw[:], w_hi[par][:], ALU.subtract).then_inc(w_split, 1)

            pool.memset(power[:], -0.5).then_inc(power_ready, 1)
            pool.memset(eps[:], EPS).then_inc(power_ready, 1)
            pool.wait_ge(power_ready, 2)
            rstd(0)
            split_weights(0, 0)
            rstd(1)
            split_tile(0)
            for t in range(2, FIRST_TILES):
                rstd(t)
                split_tile(t - 1)
            split_tile(FIRST_TILES - 1)
            split_weights(1, 1)
            pool.memset(yT[:, :, :], 0.0).then_inc(y_zeroed, 1)
            for i in range(2):
                pool.memset(v_aug[i][:, :, DH:2 * DH], 1.0).then_inc(ones_ready, 1)

            def iteration(n, par, project, prep):
                if prep:
                    rstd(n + FIRST_TILES)
                split_weights(n + 2, par)
                if prep:
                    split_tile(n + FIRST_TILES)

            iteration(0, 0, True, True)
            iteration(1, 1, True, True)
            with pool.Fori(1, NPAIR // 2 - 1) as m:
                iteration(2 * m, 0, True, True)
                iteration(2 * m + 1, 1, True, True)
            iteration(NPAIR - 2, 0, True, False)
            iteration(NPAIR - 1, 1, False, False)

        @block.tensor
        def _(pe):
            def product(out, terms):
                for i, (lhsT, rhs) in enumerate(terms):
                    mm = pe.matmul(out, lhsT, rhs, start=(i == 0), stop=(i == len(terms) - 1))
                return mm

            def split_terms(par, which, rhs_hi, rhs_lo):
                terms = []
                for k in range(KT):
                    hi, lo = w_part(w_hi[par], which, k), w_part(w_lo[par], which, k)
                    terms += [(hi, rhs_hi(k)), (hi, rhs_lo(k)), (lo, rhs_hi(k))]
                return terms

            def ctx_cols(t, p, half):
                return lambda k: t[:, bass.ds((p // PAIRS) % 2, 1), k, bass.ds(half * 512, 512)]

            def x_cols(t, p):
                return lambda k: t[:, bass.ds((p // PAIRS) % 2, 1), k, :]

            def turn_tile(t):
                wait(pe, normed, 2 * t + 2)
                for k in range(KT):
                    pe.transpose(job_ps[1][:, k * P:(k + 1) * P], ctx_n[:, k * P:(k + 1) * P], ident[:])
                for k in range(KT):
                    tr = pe.transpose(job_ps[1][:, 256 + 64 * k:320 + 64 * k], x_n[:, k * P:(k + 1) * P],
                                      ident[0:64, 0:64])
                tr.then_inc(turned, 1)

            def project_k(p, par, half):
                wait(pe, tile_split, 2 * (p + STEPS))
                wait(pe, w_split, p + 1)
                wait(pe, y_added, 2 * (p - 2) - 1 + half)
                wait(pe, v_ready, 2 * p - 1 + half)
                product(job_ps[half][:], split_terms(par, 1, ctx_cols(ctxT_hi, p, half), ctx_cols(ctxT_lo, p, half))
                        ).then_inc(k_projected, 1)

            def project_q(p, par):
                wait(pe, k_evac, 2 * p + 1)
                product(job_ps[0][:], split_terms(par, 0, x_cols(xT_hi, p), x_cols(xT_lo, p))
                        ).then_inc(q_projected, 1)

            def project_v(p, par, half):
                if half == 0:
                    wait(pe, q_split, p + 1)
                else:
                    wait(pe, k_evac, 2 * p + 2)
                product(job_ps[half][:], split_terms(par, 2, ctx_cols(ctxT_hi, p, half), ctx_cols(ctxT_lo, p, half))
                        ).then_inc(v_projected, 1)

            def turn_v(p, half):
                wait(pe, v_evac, 2 * p + 2)
                for j in range(4):
                    tr = pe.transpose(job_ps[half][:, j * P:(j + 1) * P],
                                      vT32[:, (4 * half + j) * P:(4 * half + j + 1) * P], ident[:])
                tr.then_inc(v_turned, 1)

            def project_y(n, par, bank_user):
                wait(pe, o_split, n + 1)
                wait(pe, w_split, n + 3)
                for mt in range(2):
                    if bank_user is not None:
                        wait(pe, v_ready, 2 * bank_user + 1 + mt)
                    at = 3 * KT * P + mt * P
                    hi, lo = w_hi[par][:, at:at + P], w_lo[par][:, at:at + P]
                    product(job_ps[mt][:], [(hi, o_hi[:]), (hi, o_lo[:]), (lo, o_hi[:])]).then_inc(y_projected, 1)

            def scores(n, s, par):
                g = STEPS * n + s
                h = s // 4
                if s == 0:
                    wait(pe, k_stacked, 4 * DMA * (n + 1))
                    wait(pe, q_stacked, 8 * DMA * (n + 1))
                wait(pe, exp_done, g - 1)
                for j in range(2):
                    tile = 2 * (s % 4) + j
                    keys = k_stack[par][h][:, tile * P:(tile + 1) * P]
                    mm = product(score_ps[s % 2][:, j, :], [(keys, q_hh[par][h][:]), (keys, q_ll[par][h][:])])
                mm.then_inc(scores_ready, 1)

            def attend(n, s, par):
                g = STEPS * n + s
                h = s // 4
                if s == 0:
                    wait(pe, v_ready, 2 * n + 2)
                    wait(pe, ones_ready, 2)
                if s % 4 == 0:
                    wait(pe, o_evac[h], 2 * n)
                wait(pe, clipped, g + 1)
                for j in range(2):
                    tile = 2 * (s % 4) + j
                    mm = pe.matmul(o_ps[h][:], v_aug[par][:, tile, DH * h:DH * h + P], probs[s % RING][:, j, :],
                                   start=(tile == 0), stop=(tile == S // P - 1))
                mm.then_inc(pv_done, 1)

            pe.wait_ge(ident_ready, 1)
            for t in range(FIRST_TILES):
                wait(pe, affine_done, 4 * t)
                turn_tile(t)
            project_k(0, 0, 0)
            wait(pe, affine_done, 4 * FIRST_TILES)
            project_k(0, 0, 1)
            project_q(0, 0)
            project_v(0, 0, 0)
            project_v(0, 0, 1)
            turn_v(0, 0)
            turn_v(0, 1)

            def iteration(n, par, project, prep, first=False):
                nxt = 1 - par
                for s in range(STEPS):
                    scores(n, s, par)
                    if project:
                        if s < 2:
                            project_k(n + 1, nxt, s)
                        if s == 2:
                            project_q(n + 1, nxt)
                        if s == 3:
                            if prep:
                                wait(pe, k_evac, 2 * n + 4)
                                turn_tile(n + FIRST_TILES)
                            project_v(n + 1, nxt, 0)
                        if s == 4:
                            if prep:
                                wait(pe, affine_done, 4 * (n + FIRST_TILES) + 4)
                            project_v(n + 1, nxt, 1)
                        if s in (5, 6):
                            turn_v(n + 1, s - 5)
                    if s == 7 and not first:
                        project_y(n - 1, nxt, n + 1 if project else None)
                    if s >= LAG:
                        attend(n, s - LAG, par)
                    elif not first:
                        attend(n - 1, s - LAG + STEPS, nxt)

            iteration(0, 0, True, True, first=True)
            iteration(1, 1, True, True)
            with pe.Fori(1, NPAIR // 2 - 1) as m:
                iteration(2 * m, 0, True, True)
                iteration(2 * m + 1, 1, True, True)
            iteration(NPAIR - 2, 0, True, False)
            iteration(NPAIR - 1, 1, False, False)
            for s in range(STEPS - LAG, STEPS):
                attend(NPAIR - 1, s, 1)
            wait(pe, y_added, 2 * (NPAIR - 1))
            project_y(NPAIR - 1, 1, None)

        @block.scalar
        def _(act):
            def affine(t):
                wait(act, turned, t + 1)
                wait(act, tile_split, 2 * t)
                for k in range(KT):
                    act.activation(ctx_t32[:, k, :], job_ps[1][:, k * P:(k + 1) * P], ACT.Identity,
                                   bias=b_ctx[:, k:k + 1], scale=g_ctx[:, k:k + 1]).then_inc(affine_done, 1)
                for k in range(KT):
                    act.activation(x_t32[:, k, :], job_ps[1][:, 256 + 64 * k:320 + 64 * k], ACT.Identity,
                                   bias=b_lat[:, k:k + 1], scale=g_lat[:, k:k + 1]).then_inc(affine_done, 1)

            def evac_k(p, half):
                wait(act, k_projected, 2 * p + 1 + half)
                wait(act, k_split, p)
                act.copy(k32[:, half * 512:(half + 1) * 512], job_ps[half][:]).then_inc(k_evac, 1)

            def round_q(p):
                wait(act, q_projected, p + 1)
                wait(act, q_stacked, 8 * DMA * p)
                act.copy(q_hi[:], job_ps[0][:]).then_inc(q_hi_done, 1)

            def evac_v(p, half):
                wait(act, v_projected, 2 * p + 1 + half)
                wait(act, v_turned, 2 * p)
                act.copy(vT32[:, half * 512:(half + 1) * 512], job_ps[half][:]).then_inc(v_evac, 1)

            def place_v(p, par, half):
                wait(act, v_turned, 2 * p + 1 + half)
                wait(act, pv_done, STEPS * (p - 1))
                dst = v_aug[par][:, 4 * half:4 * half + 4, :].rearrange("p t (a d) -> p t a d", a=3)
                act.copy(dst[:, :, 0:3:2, :],
                         job_ps[half][:].rearrange("p (t a d) -> p t a d", t=4, a=2)).then_inc(v_ready, 1)

            def exp(n, s):
                g = STEPS * n + s
                wait(act, scores_ready, g + 1)
                wait(act, pv_done, g - RING + 1)
                act.activation(probs[s % RING][:], score_ps[s % 2][:], ACT.Exp,
                               scale=DH ** -0.5).then_inc(exp_done, 1)

            def evac_o(n, h):
                wait(act, pv_done, STEPS * n + 4 * h + 4)
                wait(act, o_split, n)
                dst = slice(DH * h, DH * h + DH)
                other = slice(DH * (1 - h), DH * (1 - h) + DH)
                act.copy(o_raw[dst, :], o_ps[h][dst, :]).then_inc(o_evac[h], 1)
                act.copy(den[dst, :], o_ps[h][other, :]).then_inc(o_evac[h], 1)

            act.wait_ge(consts_loaded, 9 * DMA)
            for t in range(FIRST_TILES):
                affine(t)
            evac_k(0, 0)
            evac_k(0, 1)
            round_q(0)
            evac_v(0, 0)
            evac_v(0, 1)
            place_v(0, 0, 0)
            place_v(0, 0, 1)

            def iteration(n, par, project, prep, first=False):
                for s in range(STEPS):
                    exp(n, s)
                    if s == 2 and not first:
                        evac_o(n - 1, 1)
                    if project:
                        if s < 2:
                            evac_k(n + 1, s)
                        if s == 2:
                            round_q(n + 1)
                        if s == 3:
                            if prep:
                                affine(n + FIRST_TILES)
                            evac_v(n + 1, 0)
                        if s == 4:
                            evac_v(n + 1, 1)
                        if s in (5, 6):
                            place_v(n + 1, 1 - par, s - 5)
                    if s == 6:
                        evac_o(n, 0)

            iteration(0, 0, True, True, first=True)
            iteration(1, 1, True, True)
            with act.Fori(1, NPAIR // 2 - 1) as m:
                iteration(2 * m, 0, True, True)
                iteration(2 * m + 1, 1, True, True)
            iteration(NPAIR - 2, 0, True, False)
            iteration(NPAIR - 1, 1, False, False)
            evac_o(NPAIR - 1, 1)

        @block.vector
        def _(dve):
            def stats(t, slot):
                wait(dve, tile_loaded[slot], 2 * DMA * (t // 2 + 1))
                wait(dve, normed, 2 * t)
                dve.bn_stats(bn_c[:], ctx_raw[slot][:]).then_inc(bn_done, 1)
                dve.bn_stats(bn_x[:], x_raw[slot][:]).then_inc(bn_done, 1)
                dve.wait_ge(bn_done, 2 * t + 2)
                dve.tensor_copy(carry_dve[:], bn_c[:, 0:1])
                dve.bn_aggr(mv_c[:], bn_c[:]).then_inc(stats_ready, 1)
                dve.bn_aggr(mv_x[:], bn_x[:]).then_inc(stats_ready, 1)

            def normalize(t, slot):
                wait(dve, stats_ready, 2 * t + 2)
                wait(dve, rstd_ready, 2 * t + 2)
                wait(dve, turned, t)
                dve.tensor_scalar(ctx_n[:], ctx_raw[slot][:], mv_c[:, 0:1], rstd_c[:, 1:2],
                                  ALU.subtract, ALU.mult).then_inc(normed, 1)
                dve.tensor_scalar(x_n[:], x_raw[slot][:], mv_x[:, 0:1], rx[:, 6:7],
                                  ALU.subtract, ALU.mult).then_inc(normed, 1)

            def split_q(p):
                wait(dve, q_hi_done, p + 1)
                wait(dve, q_stacked, 8 * DMA * p)
                dve.tensor_tensor(q_lo[:], job_ps[0][:], q_hi[:], ALU.subtract).then_inc(q_split, 1)

            def rope_times(p):
                wait(dve, k_evac, 2 * p + 2)
                wait(dve, k_swapped, 4 * DMA * (p + 1))
                dve.tensor_tensor(k32[:], k32[:], cos_sb[:], ALU.mult).then_inc(k_times, 1)
                dve.tensor_tensor(k_swap[:], k_swap[:], sin_sb[:], ALU.mult).then_inc(k_times, 1)

            def rope_add(p):
                wait(dve, k_times, 2 * p + 2)
                dve.tensor_tensor(k32[:], k32[:], k_swap[:], ALU.add).then_inc(k_roped, 1)
                wait(dve, k_roped, p + 1)
                wait(dve, k_stacked, 4 * DMA * p)
                dve.tensor_copy(k_hi[:], k32[:]).then_inc(k_hi_done, 1)
                wait(dve, k_hi_done, p + 1)
                dve.tensor_tensor(k_lo[:], k32[:], k_hi[:], ALU.subtract).then_inc(k_split, 1)

            def clip(n, s):
                g = STEPS * n + s
                wait(dve, exp_done, g + 1)
                dve.tensor_scalar(probs[s % RING][:], probs[s % RING][:], CLIP_HI, CLIP_LO,
                                  ALU.min, ALU.max).then_inc(clipped, 1)

            def invert(n, half):
                for h in range(2):
                    wait(dve, o_evac[h], 2 * n + 2)
                part = den[:, 256 * half:256 * half + 256]
                dve.reciprocal(part, part).then_inc(den_inv, 1)

            def split_o(n):
                wait(dve, den_inv, 2 * n + 2)
                dve.tensor_tensor(o_raw[:], o_raw[:], den[:], ALU.mult).then_inc(o_scaled, 1)
                wait(dve, o_scaled, n + 1)
                wait(dve, y_projected, 2 * n)
                dve.tensor_copy(o_hi[:], o_raw[:]).then_inc(o_hi_done, 1)
                wait(dve, o_hi_done, n + 1)
                dve.tensor_tensor(o_lo[:], o_raw[:], o_hi[:], ALU.subtract).then_inc(o_split, 1)

            def add_y(n, part):
                for mt in range(2):
                    wait(dve, y_projected, 2 * n + 1 + mt)
                    wait(dve, y_added, 2 * n - 1 + mt)
                    acc = yT[:, mt, bass.ds((n // PAIRS) * NQ, NQ)]
                    dve.tensor_tensor(acc, job_ps[mt][:], acc, ALU.add).then_inc(y_added, 1)

            for t in range(FIRST_TILES):
                stats(t, t % 2)
                normalize(t, t % 2)
            dve.wait_ge(consts_loaded, 9 * DMA)
            for q in (0, 2):
                rows = slice(32 * q, 32 * q + 32)
                dve.tensor_scalar(sin_sb[rows, :], sin_sb[rows, :], -1.0, None, ALU.mult).then_inc(sin_signed, 1)
            dve.wait_ge(sin_signed, 2)
            split_q(0)
            rope_times(0)
            rope_add(0)
            dve.wait_ge(y_zeroed, 1)
            for mt in range(2):
                dve.tensor_scalar(yT[:, mt, :], yT[:, mt, :], bo[:, mt:mt + 1], None, ALU.add).then_inc(y_biased, 1)
            dve.wait_ge(y_biased, 2)

            def iteration(n, par, project, prep, first=False):
                for s in range(STEPS):
                    clip(n, s)
                    if s == 0 and prep:
                        stats(n + FIRST_TILES, 1 - par)
                    if s == 1 and prep:
                        normalize(n + FIRST_TILES, 1 - par)
                    if s in (2, 3) and not first:
                        invert(n - 1, s - 2)
                    if project:
                        if s == 3:
                            split_q(n + 1)
                        if s == 4:
                            rope_times(n + 1)
                        if s == 5:
                            rope_add(n + 1)
                    if s == 6 and not first:
                        split_o(n - 1)
                    if s == 7 and not first:
                        add_y(n - 1, par)

            iteration(0, 0, True, True, first=True)
            iteration(1, 1, True, True)
            with dve.Fori(1, NPAIR // 2 - 1) as m:
                iteration(2 * m, 0, True, True)
                iteration(2 * m + 1, 1, True, True)
            iteration(NPAIR - 2, 0, True, False)
            iteration(NPAIR - 1, 1, False, False)
            invert(NPAIR - 1, 0)
            invert(NPAIR - 1, 1)
            split_o(NPAIR - 1)
            add_y(NPAIR - 1, 1)


def ffn_phase(nc, x, selT, keys, values, sel_dram, out, yT):
    with ExitStack() as st:
        def sb(name, shape, dt=F32):
            return st.enter_context(nc.sbuf_tensor(name, shape, dt))

        def psum(name, shape):
            return st.enter_context(nc.psum_tensor(name, shape, F32))

        def sem(name):
            return st.enter_context(nc.semaphore(name))

        TILES = ALL // P
        PER = TILES // CHUNKS
        ARING = 4
        FLAG = 3
        GROUP = 4
        GROUPS = EXPERTS // GROUP

        ident = sb("ident2", [P, P])
        x2 = sb("x2", [P, TILES, D])
        sel_w = sb("sel_w", [P, KT, EXPERTS])
        sel_hi = sb("sel_hi", [P, KT, P], F32R)
        sel_lo = sb("sel_lo", [P, KT, P], F32R)
        w_raw = sb("w_raw2", [P, 2048])
        key_hi = sb("key_hi", [P, KT, EXPERTS * HID], F32R)
        key_lo = sb("key_lo", [P, KT, EXPERTS * HID], F32R)
        val_hi = sb("val_hi", [P, EXPERTS, D], F32R)
        val_lo = sb("val_lo", [P, EXPERTS, D], F32R)
        bn = sb("bn2", [P, 6])
        mv = [sb(f"mv2{i}", [P, 2]) for i in range(2)]
        rstd = [sb(f"rstd2{i}", [P, 2]) for i in range(2)]
        power = sb("power2", [P, 1])
        x_n = [sb(f"x_n2{i}", [P, D]) for i in range(2)]
        xT_hi = sb("x2T_hi", [P, KT, ALL], F32R)
        xT_lo = sb("x2T_lo", [P, KT, ALL], F32R)
        gate = [sb(f"gate{i}", [EXPERTS, 512]) for i in range(CHUNKS)]
        sel_all = [sb(f"sel_all{i}", [P, GROUP * 512]) for i in range(2)]
        act32 = [sb(f"act32{i}", [P, 512]) for i in range(ARING)]
        act_hi = [sb(f"act_hi{i}", [P, 512], F32R) for i in range(ARING)]
        act_lo = [sb(f"act_lo{i}", [P, 512], F32R) for i in range(ARING)]
        outT = sb("outT", [P, 2, 512])
        x_out = [sb(f"x_out{i}", [P, 2, D]) for i in range(2)]

        h_ps = [psum(f"h_ps{i}", [P, 512]) for i in range(ARING)]
        out_ps = [psum(f"out_ps{i}", [P, 512]) for i in range(2)]
        fin_ps = [psum(f"fin_ps{i}", [P, 2, D]) for i in range(2)]

        ident_zero = sem("ident_zero2")
        ident_ready = sem("ident_ready2")
        sel_zero = sem("sel_zero")
        x_loaded = sem("x_loaded")
        sel_w_loaded = sem("sel_w_loaded")
        raw_loaded = sem("raw_loaded")
        sel_hi_done = sem("sel_hi_done")
        sel_split = sem("sel_split")
        w_hi_done = sem("w_hi_done2")
        w_split = sem("w_split2")
        y_turned = sem("y_turned")
        fin_added = sem("fin_added")
        bn_done = sem("bn_done2")
        stats_ready = sem("stats_ready2")
        power_ready = sem("power_ready2")
        eps_added = sem("eps_added")
        rstd_ready = sem("rstd_ready2")
        normed = sem("normed2")
        x_turned = sem("x_turned")
        x_hi_done = sem("x_hi_done")
        x_split = sem("x_split")
        logits_ready = sem("logits_ready")
        gate_exp = sem("gate_exp")
        gate_plus = sem("gate_plus")
        gate_ready = sem("gate_ready")
        stored = sem("stored")
        sel_loaded = [sem(f"sel_loaded{i}") for i in range(2)]
        h_ready = sem("h_ready")
        gated = sem("gated")
        act_hi_done = sem("act_hi_done")
        act_split = sem("act_split")
        summed = sem("summed")
        out_evac = sem("out_evac")
        out_turned = sem("out_turned")

        lots = [(key_hi[:, k, :], key_lo[:, k, :]) for k in range(KT)]
        lots += [(val_hi[:, 8 * i:8 * i + 8, :].rearrange("p e d -> p (e d)"),
                  val_lo[:, 8 * i:8 * i + 8, :].rearrange("p e d -> p (e d)")) for i in range(2)]

        block = st.enter_context(nc.Block())

        @block.sync
        def _(sp):
            for q in range(4):
                sp.dma_start(x2[:, 4 * q:4 * q + 4, :],
                             x[4 * q * P:(4 * q + 4) * P, :].rearrange("(t p) d -> p t d", p=P)).then_inc(x_loaded, DMA)
                if q == 0:
                    for k in range(KT):
                        sp.dma_start(sel_w[:, k, :], selT[k * P:(k + 1) * P, :]).then_inc(sel_w_loaded, DMA)
            for lot in range(4):
                wait(sp, w_split, lot)
                if lot < 2:
                    sp.dma_start(w_raw[:].rearrange("p (e h) -> p e h", h=HID),
                                 keys[:, lot * P:(lot + 1) * P, :].rearrange("e d h -> d e h")).then_inc(raw_loaded, DMA)
                else:
                    e = 8 * (lot - 2)
                    sp.dma_start(w_raw[:].rearrange("p (e d) -> p e d", d=D),
                                 values[e:e + 8, :, :].rearrange("e h d -> h e d")).then_inc(raw_loaded, DMA)
            for c in range(CHUNKS):
                sp.wait_ge(gate_ready, c + 1)
                sp.dma_start(sel_dram[c, :, :], gate[c][:]).then_inc(stored, DMA)
            sp.wait_ge(stored, DMA * CHUNKS)

            def load_gates(c, q, slot):
                wait(sp, gated, GROUP * (GROUPS * c + q - 1))
                src = sel_dram[bass.ds(c, 1), GROUP * q:GROUP * q + GROUP, :].rearrange("a e n -> a (e n)")
                sp.dma_start(sel_all[slot][:], src[0, :].partition_broadcast(P)).then_inc(sel_loaded[slot], DMA)

            def store(c):
                for i in range(2):
                    sp.wait_ge(fin_added, TILES + 2 * c + i + 1)
                    sp.dma_start(out[bass.ds(c * 512 + i * 256, 256), :].rearrange("(t p) d -> p t d", p=P),
                                 x_out[i][:]).then_inc(stored, DMA)

            load_gates(0, 0, 0)
            load_gates(0, 1, 1)

            def chunk(c, first=False, last=False):
                load_gates(c, 2, 0)
                load_gates(c, 3, 1)
                if not first:
                    store(c - 1)
                if not last:
                    load_gates(c + 1, 0, 0)
                    load_gates(c + 1, 1, 1)

            chunk(0, first=True)
            with sp.Fori(1, CHUNKS - 1) as c:
                chunk(c)
            chunk(CHUNKS - 1, last=True)
            store(CHUNKS - 1)
            sp.wait_ge(stored, DMA * 3 * CHUNKS)

        @block.gpsimd
        def _(pool):
            pool.memset(ident[:], 0.0).then_inc(ident_zero, 1)
            pool.wait_ge(ident_zero, 1)
            pool.affine_select(out=ident[:], in_=ident[:], compare_op=ALU.not_equal, fill=1.0, base=0,
                               pattern=[[-1, P]], channel_multiplier=1).then_inc(ident_ready, 1)
            pool.memset(power[:], -0.5).then_inc(power_ready, 1)
            pool.wait_ge(power_ready, 1)
            for t in range(TILES):
                pool.wait_ge(stats_ready, t + 1)
                wait(pool, normed, t - 1)
                pool.tensor_scalar(rstd[t % 2][:, 0:1], mv[t % 2][:, 1:2], EPS, None, ALU.add).then_inc(eps_added, 1)
                pool.wait_ge(eps_added, t + 1)
                pool.tensor_tensor(rstd[t % 2][:, 1:2], rstd[t % 2][:, 0:1], power[:], ALU.pow).then_inc(rstd_ready, 1)

            def split_act(g, e):
                wait(pool, act_hi_done, g + 1)
                pool.tensor_tensor(act_lo[e % ARING][:], act32[e % ARING][:], act_hi[e % ARING][:],
                                   ALU.subtract).then_inc(act_split, 1)

            with pool.Fori(0, CHUNKS) as c:
                for e in range(EXPERTS):
                    split_act(EXPERTS * c + e, e)

        @block.tensor
        def _(pe):
            def product(out_, terms, start=True, stop=True):
                for i, (lhsT, rhs) in enumerate(terms):
                    mm = pe.matmul(out_, lhsT, rhs, start=start and i == 0, stop=stop and i == len(terms) - 1)
                return mm

            def turn_y(t):
                wait(pe, fin_added, t - 1)
                for mt in range(2):
                    tr = pe.transpose(fin_ps[t % 2][:, 0, mt * P:(mt + 1) * P], yT[:, mt, t * P:(t + 1) * P], ident[:])
                tr.then_inc(y_turned, 1)

            def turn_x(t):
                pe.wait_ge(normed, t + 1)
                wait(pe, x_split, t - 1)
                for k in range(KT):
                    tr = pe.transpose(h_ps[t % 2][:, k * P:(k + 1) * P], x_n[t % 2][:, k * P:(k + 1) * P], ident[:])
                tr.then_inc(x_turned, 1)

            def logits(c):
                pe.wait_ge(x_split, PER * (c + 1))
                pe.wait_ge(sel_split, 2)
                wait(pe, gate_exp, c - 1)
                cols_ = slice(c * 512, (c + 1) * 512)
                terms = []
                for k in range(KT):
                    terms += [(sel_hi[:, k, :], xT_hi[:, k, cols_]), (sel_hi[:, k, :], xT_lo[:, k, cols_]),
                              (sel_lo[:, k, :], xT_hi[:, k, cols_])]
                product(h_ps[2 + c % 2][:], terms).then_inc(logits_ready, 1)

            pe.wait_ge(ident_ready, 1)
            turn_y(0)
            for t in range(TILES):
                if t + 1 < TILES:
                    turn_y(t + 1)
                turn_x(t)
                if t % PER == 0 and t:
                    logits(t // PER - 1)
            logits(CHUNKS - 1)
            pe.wait_ge(x_split, TILES)
            pe.wait_ge(gate_exp, CHUNKS)
            pe.wait_ge(w_split, 4)

            def expert_in(c, g, e):
                wait(pe, gated, g - ARING + 1)
                cols_ = bass.ds(c * 512, 512)
                terms = []
                for k in range(KT):
                    hi, lo = key_hi[:, k, e * HID:(e + 1) * HID], key_lo[:, k, e * HID:(e + 1) * HID]
                    terms += [(hi, xT_hi[:, k, cols_]), (hi, xT_lo[:, k, cols_]), (lo, xT_hi[:, k, cols_])]
                product(h_ps[e % ARING][:], terms).then_inc(h_ready, 1)

            def expert_out(c, g, e):
                pe.wait_ge(act_split, g + 1)
                for mt in range(2):
                    if e == 0:
                        wait(pe, out_evac, 2 * (c - 1) + 1 + mt)
                    hi, lo = val_hi[:, e, mt * P:(mt + 1) * P], val_lo[:, e, mt * P:(mt + 1) * P]
                    mm = product(out_ps[mt][:], [(hi, act_hi[e % ARING][:]), (hi, act_lo[e % ARING][:]),
                                                 (lo, act_hi[e % ARING][:])],
                                 start=(e == 0), stop=(e == EXPERTS - 1))
                mm.then_inc(summed, 1)

            def turn_out(c):
                pe.wait_ge(out_evac, 2 * c + 2)
                for i in range(2):
                    wait(pe, fin_added, TILES + 2 * (c - 1) + 1 + i)
                    for j in range(2):
                        for mt in range(2):
                            at = (2 * i + j) * P
                            tr = pe.transpose(fin_ps[i][:, j, mt * P:(mt + 1) * P], outT[:, mt, at:at + P], ident[:])
                    tr.then_inc(out_turned, 1)

            pe.wait_ge(fin_added, TILES)

            def chunk(c, first=False):
                for e in range(EXPERTS):
                    g = EXPERTS * c + e
                    expert_in(c, g, e)
                    if e >= FLAG:
                        expert_out(c, g - FLAG, e - FLAG)
                    elif not first:
                        expert_out(c - 1, g - FLAG, e - FLAG + EXPERTS)
                    if e == 5 and not first:
                        turn_out(c - 1)

            chunk(0, first=True)
            with pe.Fori(1, CHUNKS) as c:
                chunk(c)
            for e in range(EXPERTS - FLAG, EXPERTS):
                expert_out(CHUNKS - 1, EXPERTS * (CHUNKS - 1) + e, e)
            turn_out(CHUNKS - 1)

        @block.scalar
        def _(act):
            def round_x(t):
                act.wait_ge(x_turned, t + 1)
                dst = xT_hi[:, :, t * P:(t + 1) * P]
                act.copy(dst, h_ps[t % 2][:, 0:KT * P].rearrange("p (k n) -> p k n", k=KT)).then_inc(x_hi_done, 1)

            def exp_gate(c):
                act.wait_ge(logits_ready, c + 1)
                act.activation(gate[c][:], h_ps[2 + c % 2][0:EXPERTS, :], ACT.Exp, scale=-1.0).then_inc(gate_exp, 1)

            def round_weights(lot):
                act.wait_ge(raw_loaded, DMA * (lot + 1))
                act.copy(lots[lot][0], w_raw[:]).then_inc(w_hi_done, 1)

            for t in range(TILES):
                round_x(t)
                if t % PER == 0 and t:
                    round_weights(t // PER - 1)
                    if t // PER >= 2:
                        exp_gate(t // PER - 2)
            round_weights(3)
            exp_gate(CHUNKS - 2)
            exp_gate(CHUNKS - 1)

            def round_act(g, e):
                act.wait_ge(gated, g + 1)
                wait(act, summed, g - ARING + 1)
                act.copy(act_hi[e % ARING][:], act32[e % ARING][:]).then_inc(act_hi_done, 1)

            def evac_out(c):
                act.wait_ge(summed, EXPERTS * (c + 1))
                for mt in range(2):
                    act.copy(outT[:, mt, :], out_ps[mt][:]).then_inc(out_evac, 1)

            def chunk(c, first=False):
                for e in range(EXPERTS):
                    if e == FLAG and not first:
                        evac_out(c - 1)
                    round_act(EXPERTS * c + e, e)

            chunk(0, first=True)
            with act.Fori(1, CHUNKS) as c:
                chunk(c)
            evac_out(CHUNKS - 1)

        @block.vector
        def _(dve):
            def residual(t):
                dve.wait_ge(y_turned, t + 1)
                if t % 4 == 0:
                    dve.wait_ge(x_loaded, DMA * 4)
                dve.tensor_tensor(x2[:, t, :], fin_ps[t % 2][:, 0, :], x2[:, t, :], ALU.add).then_inc(fin_added, 1)
                dve.wait_ge(fin_added, t + 1)
                wait(dve, stats_ready, t)
                dve.bn_stats(bn[:], x2[:, t, :]).then_inc(bn_done, 1)
                dve.wait_ge(bn_done, t + 1)
                dve.bn_aggr(mv[t % 2][:], bn[:]).then_inc(stats_ready, 1)

            def normalize(t):
                dve.wait_ge(rstd_ready, t + 1)
                wait(dve, x_turned, t - 1)
                dve.tensor_scalar(x_n[t % 2][:], x2[:, t, :], mv[t % 2][:, 0:1], rstd[t % 2][:, 1:2],
                                  ALU.subtract, ALU.mult).then_inc(normed, 1)

            def split_x(t):
                dve.wait_ge(x_hi_done, t + 1)
                dve.tensor_tensor(xT_lo[:, :, t * P:(t + 1) * P],
                                  h_ps[t % 2][:, 0:KT * P].rearrange("p (k n) -> p k n", k=KT),
                                  xT_hi[:, :, t * P:(t + 1) * P], ALU.subtract).then_inc(x_split, 1)

            def split_weights(lot):
                dve.wait_ge(w_hi_done, lot + 1)
                dve.tensor_tensor(lots[lot][1], w_raw[:], lots[lot][0], ALU.subtract).then_inc(w_split, 1)

            def invert_gate(c):
                dve.wait_ge(gate_exp, c + 1)
                dve.tensor_scalar(gate[c][:], gate[c][:], 1.0, None, ALU.add).then_inc(gate_plus, 1)
                dve.wait_ge(gate_plus, c + 1)
                dve.reciprocal(gate[c][:], gate[c][:]).then_inc(gate_ready, 1)

            dve.memset(raw(sel_hi), 0.0).then_inc(sel_zero, 1)
            dve.memset(raw(sel_lo), 0.0).then_inc(sel_zero, 1)
            dve.wait_ge(sel_zero, 2)
            dve.wait_ge(sel_w_loaded, 2 * DMA)
            dve.tensor_copy(sel_hi[:, :, 0:EXPERTS], sel_w[:]).then_inc(sel_hi_done, 1)
            dve.wait_ge(sel_hi_done, 1)
            dve.tensor_tensor(sel_lo[:, :, 0:EXPERTS], sel_w[:], sel_hi[:, :, 0:EXPERTS],
                              ALU.subtract).then_inc(sel_split, 2)
            residual(0)
            for t in range(TILES):
                if t + 1 < TILES:
                    residual(t + 1)
                normalize(t)
                if t:
                    split_x(t - 1)
                    if t % PER == 0:
                        if t // PER >= 2:
                            split_weights(t // PER - 2)
                        if t // PER >= 3:
                            invert_gate(t // PER - 3)
            split_x(TILES - 1)
            split_weights(2)
            split_weights(3)
            for c in range(1, CHUNKS):
                invert_gate(c)

            def gate_h(c, e):
                g = EXPERTS * c + e
                dve.wait_ge(h_ready, g + 1)
                q = e // GROUP
                if e % GROUP == 0:
                    wait(dve, sel_loaded[q % 2], DMA * (2 * c + q // 2 + 1))
                wait(dve, act_split, g - ARING + 1)
                at = (e % GROUP) * 512
                dve.scalar_tensor_tensor(out=act32[e % ARING][:], in0=h_ps[e % ARING][:], scalar=0.0,
                                         in1=sel_all[q % 2][:, at:at + 512], op0=ALU.max, op1=ALU.mult
                                         ).then_inc(gated, 1)

            def add_out(c):
                for i in range(2):
                    dve.wait_ge(out_turned, 2 * c + i + 1)
                    dve.wait_ge(stored, DMA * (CHUNKS + 2 * c))
                    dve.tensor_tensor(x_out[i][:], fin_ps[i][:], x2[:, bass.ds(c * PER + 2 * i, 2), :],
                                      ALU.add).then_inc(fin_added, 1)

            def chunk(c, first=False):
                for e in range(EXPERTS):
                    gate_h(c, e)
                    if e == 6 and not first:
                        add_out(c - 1)

            chunk(0, first=True)
            with dve.Fori(1, CHUNKS) as c:
                chunk(c)
            add_out(CHUNKS - 1)


def build(nc, x, ctx_in, cosT, sinT, cols, Wq, Wkv, Wo, selT, keys, values, out, sel_dram):
    with ExitStack() as st:
        yT = st.enter_context(nc.sbuf_tensor("yT", [P, 2, ALL], F32))
        attention_phase(nc, x, ctx_in, cosT, sinT, cols, Wq, Wkv, Wo, yT)
        ffn_phase(nc, x, selT, keys, values, sel_dram, out, yT)


def kernel(x, ctx_1024, L0_xattn_cos, L0_xattn_sin, L0_xattn_ln_lat_g, L0_xattn_ln_lat_b, L0_xattn_ln_ctx_g,
           L0_xattn_ln_ctx_b, L0_xattn_Wq, L0_xattn_Wkv, L0_xattn_Wo, L0_xattn_bo, L0_ffn_expert_sel,
           L0_ffn_keys, L0_ffn_values):
    import numpy as np
    import concourse.bacc as bacc
    from concourse.bass_utils import run_bass_kernel_spmd

    vectors = [L0_xattn_ln_lat_g, L0_xattn_ln_lat_b, L0_xattn_ln_ctx_g, L0_xattn_ln_ctx_b, L0_xattn_bo]
    cols = np.concatenate([np.asarray(v).reshape(KT, P) for v in vectors], axis=0).T
    arrays = {
        "x": np.asarray(x).reshape(ALL, D),
        "ctx": np.asarray(ctx_1024).reshape(B * S, D),
        "cosT": np.asarray(L0_xattn_cos).T,
        "sinT": np.asarray(L0_xattn_sin).T,
        "cols": cols,
        "Wq": L0_xattn_Wq,
        "Wkv": L0_xattn_Wkv,
        "Wo": L0_xattn_Wo,
        "selT": np.asarray(L0_ffn_expert_sel).T,
        "keys": L0_ffn_keys,
        "values": L0_ffn_values,
    }
    arrays = {name: np.ascontiguousarray(a) for name, a in arrays.items()}
    nc = bacc.Bacc("TRN2", target_bir_lowering=False, num_devices=1)
    ins = [nc.dram_tensor(name, a.shape, mybir.dt.from_np(a.dtype), kind="ExternalInput").ap()
           for name, a in arrays.items()]
    out = nc.dram_tensor("out", (ALL, D), F32, kind="ExternalOutput").ap()
    sel_dram = nc.dram_tensor("sel_dram", (CHUNKS, EXPERTS, 512), F32, kind="Internal").ap()
    build(nc, *ins, out, sel_dram)
    r = run_bass_kernel_spmd(nc, [arrays], core_ids=[0])
    return r.results[0]["out"].reshape(B, NQ, D)
```

```python
from contextlib import ExitStack

import concourse.bass as bass
from concourse import mybir

F32 = mybir.dt.float32
F32R = mybir.dt.float32r
ALU = mybir.AluOpType
ACT = mybir.ActivationFunctionType

P = 128
DMA = 16
B, NQ, D = 4, 512, 256
S = 1024
HEADS, DH = 16, 64
INNER = HEADS * DH
KT = D // P
PAIRS = HEADS // 2
NPAIR = B * PAIRS
STEPS = 8
ALL = B * NQ
EXPERTS, HID = 16, 128
CHUNKS = ALL // 512
EPS = 1e-5
CLIP_HI = 59874.141715197816
CLIP_LO = 1.670170079024566e-05
FIRST_TILES = 9
LAG = 2
POOL_STEPS = (2, 4, 6)
DVE_STEPS = (0, 1, 3, 5, 7)


def wait(eng, sem, value):
    if isinstance(value, int) and value <= 0:
        return
    eng.wait_ge(sem, value)


def raw(t):
    return t[:].bitcast(F32)


def attention_phase(nc, x, ctx_in, cosT, sinT, cols, Wq, Wkv, Wo, yT):
    with ExitStack() as st:
        def sb(name, shape, dt=F32):
            return st.enter_context(nc.sbuf_tensor(name, shape, dt))

        def psum(name, shape):
            return st.enter_context(nc.psum_tensor(name, shape, F32))

        def sem(name):
            return st.enter_context(nc.semaphore(name))

        ident = sb("ident", [P, P])
        cos_sb = sb("cos_sb", [P, S])
        sin_sb = sb("sin_sb", [P, S])
        col_sb = sb("col_sb", [P, 10])
        ctx_raw = [sb(f"ctx_raw{i}", [P, D]) for i in range(2)]
        x_raw = [sb(f"x_raw{i}", [64, D]) for i in range(2)]
        bn_c = sb("bn_c", [P, 6])
        bn_x = sb("bn_x", [64, 6])
        mv_c = [sb(f"mv_c{i}", [P, 2]) for i in range(2)]
        mv_x = [sb(f"mv_x{i}", [64, 2]) for i in range(2)]
        var_sb = [sb(f"var_sb{i}", [P, 2]) for i in range(2)]
        rstd_sb = [sb(f"rstd_sb{i}", [P, 2]) for i in range(2)]
        power = sb("power", [P, 2])
        carry_pool = sb("carry_pool", [P, 2])
        carry_dve = sb("carry_dve", [P, 1])
        ctx_n = sb("ctx_n", [P, D])
        x_n = sb("x_n", [64, D])
        ctx_t32 = sb("ctx_t32", [P, KT, P])
        x_t32 = sb("x_t32", [P, KT, 64])
        ctxT_hi = sb("ctxT_hi", [P, 2, KT, S], F32R)
        ctxT_lo = sb("ctxT_lo", [P, 2, KT, S], F32R)
        xT_hi = sb("xT_hi", [P, 2, KT, NQ], F32R)
        xT_lo = sb("xT_lo", [P, 2, KT, NQ], F32R)
        WC = 3 * KT * P + D
        w_raw = sb("w_raw", [P, WC])
        w_hi = [sb(f"w_hi{i}", [P, WC], F32R) for i in range(2)]
        w_lo = [sb(f"w_lo{i}", [P, WC], F32R) for i in range(2)]
        k32 = sb("k32", [P, S])
        k_swap = sb("k_swap", [P, S])
        k_stack = [[sb(f"k_stack{i}{h}", [P, S], F32R) for h in range(2)] for i in range(2)]
        q_hi = sb("q_hi", [P, NQ], F32R)
        q_lo = sb("q_lo", [P, NQ], F32R)
        q_hh = [sb(f"q_hh{h}", [P, NQ], F32R) for h in range(2)]
        q_ll = [sb(f"q_ll{h}", [P, NQ], F32R) for h in range(2)]
        vT32 = sb("vT32", [P, S])
        v_hi = [sb(f"v_hi{i}", [P, S // P * 3 * DH], F32R) for i in range(2)]
        v_lo = [sb(f"v_lo{i}", [P, S // P * 3 * DH], F32R) for i in range(2)]
        probs = [sb(f"probs{i}", [P, 2, NQ]) for i in range(2)]
        p_hi = [sb(f"p_hi{i}", [P, 2, NQ], F32R) for i in range(2)]
        p_lo = [sb(f"p_lo{i}", [P, 2, NQ], F32R) for i in range(2)]
        o_raw = sb("o_raw", [P, NQ])
        den = sb("den", [P, NQ])
        o_hi = sb("o_hi", [P, NQ], F32R)
        o_lo = sb("o_lo", [P, NQ], F32R)

        score_ps = [psum(f"score_ps{i}", [P, 2, NQ]) for i in range(2)]
        o_ps = [psum(f"o_ps{h}", [P, NQ]) for h in range(2)]
        job_ps = [psum(f"job_ps{i}", [P, 512]) for i in range(2)]

        consts_loaded = sem("consts_loaded")
        ident_zero = sem("ident_zero")
        ident_ready = sem("ident_ready")
        sin_signed = sem("sin_signed")
        y_zeroed = sem("y_zeroed")
        y_biased = sem("y_biased")
        ones_ready = sem("ones_ready")
        tile_loaded = [sem(f"tile_loaded{i}") for i in range(2)]
        bn_done = sem("bn_done")
        stats_ready = sem("stats_ready")
        aggregated = sem("aggregated")
        power_ready = sem("power_ready")
        rstd_ready = sem("rstd_ready")
        normed = sem("normed")
        turned = sem("turned")
        affine_done = sem("affine_done")
        tile_hi = sem("tile_hi")
        tile_split = sem("tile_split")
        w_loaded = sem("w_loaded")
        w_hi_done = sem("w_hi_done")
        w_split = sem("w_split")
        k_projected = sem("k_projected")
        k_evac = sem("k_evac")
        k_swapped = sem("k_swapped")
        k_times = sem("k_times")
        k_roped = sem("k_roped")
        k_hi_done = sem("k_hi_done")
        k_split = sem("k_split")
        q_projected = sem("q_projected")
        q_hi_done = sem("q_hi_done")
        q_split = sem("q_split")
        q_stacked = [sem("q_stacked_a"), sem("q_stacked_b")]
        v_projected = sem("v_projected")
        v_evac = sem("v_evac")
        v_turned = sem("v_turned")
        v_hi_done = sem("v_hi_done")
        v_split = sem("v_split")
        scores_ready = sem("scores_ready")
        exp_done = sem("exp_done")
        clipped = sem("clipped")
        p_hi_done = sem("p_hi_done")
        p_split_dve = sem("p_split_dve")
        p_split_pool = sem("p_split_pool")
        pv_done = sem("pv_done")
        o_evac = [sem("o_evac_a"), sem("o_evac_b")]
        den_inv = sem("den_inv")
        o_scaled = sem("o_scaled")
        o_hi_done = sem("o_hi_done")
        o_split = sem("o_split")
        y_projected = sem("y_projected")
        y_added = sem("y_added")

        g_lat, b_lat, g_ctx, b_ctx, bo = (col_sb[:, 2 * i:2 * i + 2] for i in range(5))

        def v_part(v, tiles):
            return v[:, tiles.start * 3 * DH:tiles.stop * 3 * DH].rearrange("p (t a d) -> p t a d", a=3, d=DH)[:, :, 0:3:2, :]

        def wait_split(eng, n, s):
            if s < 0:
                n, s = n - 1, s + STEPS
            if s in POOL_STEPS:
                wait(eng, p_split_pool, len(POOL_STEPS) * n + POOL_STEPS.index(s) + 1)
            else:
                wait(eng, p_split_dve, len(DVE_STEPS) * n + DVE_STEPS.index(s) + 1)

        def w_part(w, which, k):
            at = (which * KT + k) * P
            return w[:, at:at + P]

        block = st.enter_context(nc.Block())

        @block.sync
        def _(sp):
            def load_tile(t):
                slot = t % 2 if isinstance(t, int) else t_slot[0]
                tt = t % (B * STEPS)
                sp.dma_start(ctx_raw[slot][:], ctx_in[bass.ds(tt * P, P), :]).then_inc(tile_loaded[slot], DMA)
                sp.dma_start(x_raw[slot][:], x[bass.ds(tt * 64, 64), :]).then_inc(tile_loaded[slot], DMA)

            t_slot = [0]

            def load_weights(w, has_wo=True):
                wait(sp, w_split, w)
                p = w % PAIRS
                for which, src, off in ((0, Wq, 0), (1, Wkv, 0), (2, Wkv, INNER)):
                    at = which * KT * P
                    sp.dma_start(
                        w_raw[:, at:at + KT * P].rearrange("c (k n) -> c k n", k=KT),
                        src[:, bass.ds(p * P + off, P)].rearrange("(k c) n -> c k n", k=KT),
                    ).then_inc(w_loaded, DMA)
                pw = (w + PAIRS - 2) % PAIRS
                sp.dma_start(w_raw[:, 3 * KT * P:], Wo[bass.ds(pw * P, P), :]).then_inc(w_loaded, DMA)

            def swap_k(p):
                wait(sp, k_evac, 2 * p + 2)
                wait(sp, k_roped, p)
                for q in range(4):
                    a, b = 32 * q, 32 * (q ^ 1)
                    sp.dma_start(k_swap[a:a + 32, :], k32[b:b + 32, :]).then_inc(k_swapped, DMA)

            def stack_q(p, h):
                wait(sp, scores_ready, STEPS * (p - 1) + 4 * (h + 1))
                src = slice(DH * h, DH * h + DH)
                for half in range(2):
                    dst = slice(DH * half, DH * half + DH)
                    sp.dma_start(raw(q_hh[h])[dst, :], raw(q_hi)[src, :]).then_inc(q_stacked[h], DMA)
                    sp.dma_start(raw(q_ll[h])[dst, :], raw(q_lo)[src, :]).then_inc(q_stacked[h], DMA)

            load_tile(0)
            load_weights(0)
            for q in range(4):
                rows = slice(32 * q, 32 * q + 32)
                sp.dma_start(cos_sb[rows, :], cosT).then_inc(consts_loaded, DMA)
                sp.dma_start(sin_sb[rows, :], sinT).then_inc(consts_loaded, DMA)
            sp.dma_start(col_sb[:], cols).then_inc(consts_loaded, DMA)
            load_tile(1)
            load_weights(1)
            for t in range(2, FIRST_TILES + 1):
                sp.wait_ge(normed, 2 * (t - 1))
                load_tile(t)
            load_weights(2)
            swap_k(0)
            sp.wait_ge(q_split, 1)
            stack_q(0, 0)
            stack_q(0, 1)

            def iteration(n, par, project, prep):
                if project:
                    swap_k(n + 1)
                    wait(sp, q_split, n + 2)
                if prep:
                    t_slot[0] = par
                    load_tile(n + FIRST_TILES + 1)
                if project:
                    stack_q(n + 1, 0)
                    load_weights(n + 3)
                    stack_q(n + 1, 1)

            iteration(0, 0, True, True)
            iteration(1, 1, True, True)
            with sp.Fori(1, NPAIR // 2 - 1) as m:
                iteration(2 * m, 0, True, True)
                iteration(2 * m + 1, 1, True, True)
            iteration(NPAIR - 2, 0, True, False)

        @block.gpsimd
        def _(pool):
            pool.memset(ident[:], 0.0).then_inc(ident_zero, 1)
            pool.wait_ge(ident_zero, 1)
            pool.affine_select(out=ident[:], in_=ident[:], compare_op=ALU.not_equal, fill=1.0, base=0,
                               pattern=[[-1, P]], channel_multiplier=1).then_inc(ident_ready, 1)

            def rstd(t, slot):
                wait(pool, stats_ready, 2 * t + 2)
                wait(pool, normed, 2 * (t - 1))
                pool.tensor_tensor(rstd_sb[slot][:], var_sb[slot][:], power[:], ALU.pow).then_inc(rstd_ready, 1)

            def split_tile(t):
                wait(pool, affine_done, 4 * t + 4)
                bp = (t // STEPS) % 2
                cs = t % STEPS
                c_hi = ctxT_hi[:, bass.ds(bp, 1), :, bass.ds(cs * P, P)]
                c_lo = ctxT_lo[:, bass.ds(bp, 1), :, bass.ds(cs * P, P)]
                x_hi = xT_hi[:, bass.ds(bp, 1), :, bass.ds(cs * 64, 64)]
                x_lo = xT_lo[:, bass.ds(bp, 1), :, bass.ds(cs * 64, 64)]
                c32 = ctx_t32[:, :, :].rearrange("p (a k) n -> p a k n", a=1)
                x32 = x_t32[:, :, :].rearrange("p (a k) n -> p a k n", a=1)
                pool.tensor_copy(c_hi, c32).then_inc(tile_hi, 1)
                pool.tensor_copy(x_hi, x32).then_inc(tile_hi, 1)
                pool.wait_ge(tile_hi, 2 * t + 2)
                pool.tensor_tensor(c_lo, c32, c_hi, ALU.subtract).then_inc(tile_split, 1)
                pool.tensor_tensor(x_lo, x32, x_hi, ALU.subtract).then_inc(tile_split, 1)

            def round_weights(w, par):
                wait(pool, w_loaded, 4 * DMA * (w + 1))
                wait(pool, v_projected, 2 * (w - 1))
                wait(pool, y_projected, 2 * (w - 3))
                pool.tensor_tensor(carry_pool[:], power[:], power[:], ALU.add)
                pool.tensor_copy(w_hi[par][:], w_raw[:]).then_inc(w_hi_done, 1)

            def split_weights(w, par):
                pool.wait_ge(w_hi_done, w + 1)
                pool.tensor_tensor(w_lo[par][:], w_raw[:], w_hi[par][:], ALU.subtract).then_inc(w_split, 1)

            for slot in range(2):
                pool.memset(var_sb[slot][:], 1.0).then_inc(power_ready, 1)
            pool.memset(power[:], -0.5).then_inc(power_ready, 1)
            pool.wait_ge(power_ready, 3)
            for t in range(FIRST_TILES):
                rstd(t, t % 2)
            pool.memset(yT[:, :, :], 0.0).then_inc(y_zeroed, 1)
            for v, fill in ((v_hi, 1.0), (v_lo, 0.0)):
                for i in range(2):
                    middle = raw(v[i]).rearrange("p (t a d) -> p t a d", a=3, d=DH)[:, :, 1, :]
                    pool.memset(middle, fill).then_inc(ones_ready, 1)

            def split_probs(n, s):
                wait(pool, p_hi_done, STEPS * n + s + 1)
                pool.tensor_tensor(p_lo[s % 2][:], probs[s % 2][:], p_hi[s % 2][:],
                                   ALU.subtract).then_inc(p_split_pool, 1)

            def iteration(n, par, project, prep):
                if prep:
                    rstd(n + FIRST_TILES, 1 - par)
                split_probs(n, 2)
                round_weights(n + 2, par)
                split_probs(n, 4)
                split_weights(n + 2, par)
                if prep:
                    split_tile(n + FIRST_TILES)
                split_probs(n, 6)

            iteration(0, 0, True, True)
            iteration(1, 1, True, True)
            with pool.Fori(1, NPAIR // 2 - 1) as m:
                iteration(2 * m, 0, True, True)
                iteration(2 * m + 1, 1, True, True)
            iteration(NPAIR - 2, 0, True, False)
            iteration(NPAIR - 1, 1, False, False)

        @block.tensor
        def _(pe):
            def product(out, terms, start=True, stop=True):
                for i, (lhsT, rhs) in enumerate(terms):
                    mm = pe.matmul(out, lhsT, rhs, start=start and i == 0, stop=stop and i == len(terms) - 1)
                return mm

            def split_terms(par, which, rhs_hi, rhs_lo):
                terms = []
                for k in range(KT):
                    hi, lo = w_part(w_hi[par], which, k), w_part(w_lo[par], which, k)
                    terms += [(hi, rhs_hi(k)), (hi, rhs_lo(k)), (lo, rhs_hi(k))]
                return terms

            def ctx_cols(t, p, half):
                return lambda k: t[:, bass.ds((p // PAIRS) % 2, 1), k, bass.ds(half * 512, 512)]

            def x_cols(t, p):
                return lambda k: t[:, bass.ds((p // PAIRS) % 2, 1), k, :]

            def turn_tile(t):
                wait(pe, normed, 2 * t + 2)
                for k in range(KT):
                    pe.transpose(job_ps[1][:, k * P:(k + 1) * P], ctx_n[:, k * P:(k + 1) * P], ident[:])
                for k in range(KT):
                    tr = pe.transpose(job_ps[1][:, 256 + 64 * k:320 + 64 * k], x_n[:, k * P:(k + 1) * P],
                                      ident[0:64, 0:64])
                tr.then_inc(turned, 1)

            def project_k(p, par, half):
                wait(pe, tile_split, 2 * (p + STEPS))
                wait(pe, w_split, p + 1)
                wait(pe, y_added, 2 * (p - 2) - 1 + half)
                wait(pe, v_split, 2 * p - 1 + half)
                product(job_ps[half][:], split_terms(par, 1, ctx_cols(ctxT_hi, p, half), ctx_cols(ctxT_lo, p, half))
                        ).then_inc(k_projected, 1)

            def project_q(p, par):
                wait(pe, k_evac, 2 * p + 1)
                product(job_ps[0][:], split_terms(par, 0, x_cols(xT_hi, p), x_cols(xT_lo, p))
                        ).then_inc(q_projected, 1)

            def project_v(p, par, half):
                if half == 0:
                    wait(pe, q_split, p + 1)
                else:
                    wait(pe, k_evac, 2 * p + 2)
                product(job_ps[half][:], split_terms(par, 2, ctx_cols(ctxT_hi, p, half), ctx_cols(ctxT_lo, p, half))
                        ).then_inc(v_projected, 1)

            def turn_v(p, half):
                wait(pe, v_evac, 2 * p + 2)
                for j in range(4):
                    tr = pe.transpose(job_ps[half][:, j * P:(j + 1) * P],
                                      vT32[:, (4 * half + j) * P:(4 * half + j + 1) * P], ident[:])
                tr.then_inc(v_turned, 1)

            def project_y(n, par, bank_user):
                wait(pe, o_split, n + 1)
                wait(pe, w_split, n + 3)
                for mt in range(2):
                    if bank_user is not None:
                        wait(pe, v_split, 2 * bank_user + 1 + mt)
                    at = 3 * KT * P + mt * P
                    hi, lo = w_hi[par][:, at:at + P], w_lo[par][:, at:at + P]
                    product(job_ps[mt][:], [(hi, o_hi[:]), (hi, o_lo[:]), (lo, o_hi[:])]).then_inc(y_projected, 1)

            def scores(n, s, par):
                g = STEPS * n + s
                h = s // 4
                if s == 0:
                    wait(pe, k_split, 2 * n + 2)
                if s % 4 == 0:
                    wait(pe, q_stacked[h], 4 * DMA * (n + 1))
                wait(pe, exp_done, g - 1)
                for j in range(2):
                    tile = 2 * (s % 4) + j
                    keys = k_stack[par][h][:, tile * P:(tile + 1) * P]
                    mm = product(score_ps[s % 2][:, j, :], [(keys, q_hh[h][:]), (keys, q_ll[h][:])])
                mm.then_inc(scores_ready, 1)

            def attend(n, s, par):
                g = STEPS * n + s
                h = s // 4
                if s == 0:
                    wait(pe, v_split, 2 * n + 2)
                    wait(pe, ones_ready, 4)
                if s % 4 == 0:
                    wait(pe, o_evac[h], 2 * n)
                wait_split(pe, n, s)
                for j in range(2):
                    tile = 2 * (s % 4) + j
                    at = tile * 3 * DH + DH * h
                    hi, lo = v_hi[par][:, at:at + P], v_lo[par][:, at:at + P]
                    terms = [(hi, p_hi[s % 2][:, j, :]), (hi, p_lo[s % 2][:, j, :]), (lo, p_hi[s % 2][:, j, :])]
                    mm = product(o_ps[h][:], terms, start=(tile == 0), stop=(tile == S // P - 1))
                mm.then_inc(pv_done, 1)

            pe.wait_ge(ident_ready, 1)
            for t in range(FIRST_TILES):
                wait(pe, affine_done, 4 * t)
                turn_tile(t)
            project_k(0, 0, 0)
            wait(pe, affine_done, 4 * FIRST_TILES)
            project_k(0, 0, 1)
            project_q(0, 0)
            project_v(0, 0, 0)
            project_v(0, 0, 1)
            turn_v(0, 0)
            turn_v(0, 1)

            def iteration(n, par, project, prep, first=False):
                nxt = 1 - par
                for s in range(STEPS):
                    scores(n, s, par)
                    if project:
                        if s < 2:
                            project_k(n + 1, nxt, s)
                        if s == 2:
                            project_q(n + 1, nxt)
                        if s == 3:
                            if prep:
                                wait(pe, k_evac, 2 * n + 4)
                                turn_tile(n + FIRST_TILES)
                            project_v(n + 1, nxt, 0)
                        if s == 4:
                            if prep:
                                wait(pe, affine_done, 4 * (n + FIRST_TILES) + 4)
                            project_v(n + 1, nxt, 1)
                        if s in (5, 6):
                            turn_v(n + 1, s - 5)
                    if s == 7 and not first:
                        project_y(n - 1, nxt, n + 1 if project else None)
                    if s >= LAG:
                        attend(n, s - LAG, par)
                    elif not first:
                        attend(n - 1, s - LAG + STEPS, nxt)

            iteration(0, 0, True, True, first=True)
            iteration(1, 1, True, True)
            with pe.Fori(1, NPAIR // 2 - 1) as m:
                iteration(2 * m, 0, True, True)
                iteration(2 * m + 1, 1, True, True)
            iteration(NPAIR - 2, 0, True, False)
            iteration(NPAIR - 1, 1, False, False)
            for s in range(STEPS - LAG, STEPS):
                attend(NPAIR - 1, s, 1)
            wait(pe, y_added, 2 * (NPAIR - 1))
            project_y(NPAIR - 1, 1, None)

        @block.scalar
        def _(act):
            def affine(t):
                wait(act, turned, t + 1)
                wait(act, tile_split, 2 * t)
                for k in range(KT):
                    act.activation(ctx_t32[:, k, :], job_ps[1][:, k * P:(k + 1) * P], ACT.Identity,
                                   bias=b_ctx[:, k:k + 1], scale=g_ctx[:, k:k + 1]).then_inc(affine_done, 1)
                for k in range(KT):
                    act.activation(x_t32[:, k, :], job_ps[1][:, 256 + 64 * k:320 + 64 * k], ACT.Identity,
                                   bias=b_lat[:, k:k + 1], scale=g_lat[:, k:k + 1]).then_inc(affine_done, 1)

            def evac_k(p, half):
                wait(act, k_projected, 2 * p + 1 + half)
                wait(act, k_split, 2 * p)
                act.copy(k32[:, half * 512:(half + 1) * 512], job_ps[half][:]).then_inc(k_evac, 1)

            def round_q(p):
                wait(act, q_projected, p + 1)
                for h in range(2):
                    wait(act, q_stacked[h], 4 * DMA * p)
                act.copy(q_hi[:], job_ps[0][:]).then_inc(q_hi_done, 1)

            def evac_v(p, half):
                wait(act, v_projected, 2 * p + 1 + half)
                wait(act, v_turned, 2 * p)
                act.copy(vT32[:, half * 512:(half + 1) * 512], job_ps[half][:]).then_inc(v_evac, 1)

            def round_v(p, par, half):
                wait(act, v_turned, 2 * p + 1 + half)
                wait(act, pv_done, STEPS * (p - 1))
                act.copy(v_part(v_hi[par], slice(4 * half, 4 * half + 4)),
                         job_ps[half][:].rearrange("p (t a d) -> p t a d", t=4, a=2)).then_inc(v_hi_done, 1)

            def round_k(p, par, h):
                wait(act, k_roped, p + 1)
                wait(act, scores_ready, STEPS * (p - 1))
                rows = slice(DH * h, DH * h + DH)
                act.copy(k_stack[par][h][rows, :], k32[rows, :]).then_inc(k_hi_done, 1)

            def exp(n, s):
                g = STEPS * n + s
                wait(act, scores_ready, g + 1)
                wait_split(act, n, s - 2)
                act.activation(probs[s % 2][:], score_ps[s % 2][:], ACT.Exp, scale=DH ** -0.5).then_inc(exp_done, 1)

            def round_probs(n, s):
                g = STEPS * n + s
                wait(act, clipped, g + 1)
                wait(act, pv_done, g - 1)
                act.copy(p_hi[s % 2][:], probs[s % 2][:]).then_inc(p_hi_done, 1)

            def evac_o(n, h):
                wait(act, pv_done, STEPS * n + 4 * h + 4)
                wait(act, o_split, n)
                dst = slice(DH * h, DH * h + DH)
                other = slice(DH * (1 - h), DH * (1 - h) + DH)
                act.copy(o_raw[dst, :], o_ps[h][dst, :]).then_inc(o_evac[h], 1)
                act.copy(den[dst, :], o_ps[h][other, :]).then_inc(o_evac[h], 1)

            def round_weights(w, par):
                act.wait_ge(w_loaded, 4 * DMA * (w + 1))
                act.copy(w_hi[par][:], w_raw[:]).then_inc(w_hi_done, 1)

            round_weights(0, 0)
            act.wait_ge(consts_loaded, 9 * DMA)
            for t in range(FIRST_TILES):
                affine(t)
                if t == 1:
                    round_weights(1, 1)
            evac_k(0, 0)
            evac_k(0, 1)
            round_q(0)
            evac_v(0, 0)
            evac_v(0, 1)
            round_v(0, 0, 0)
            round_v(0, 0, 1)
            round_k(0, 0, 0)
            round_k(0, 0, 1)

            def iteration(n, par, project, prep, first=False):
                for s in range(STEPS):
                    exp(n, s)
                    if project:
                        if s < 2:
                            evac_k(n + 1, s)
                        if s == 2:
                            round_q(n + 1)
                        if s == 3:
                            if prep:
                                affine(n + FIRST_TILES)
                            evac_v(n + 1, 0)
                        if s == 4:
                            evac_v(n + 1, 1)
                        if s in (5, 6):
                            round_v(n + 1, 1 - par, s - 5)
                            round_k(n + 1, 1 - par, s - 5)
                    if s == 2 and not first:
                        evac_o(n - 1, 1)
                    if s == 7:
                        evac_o(n, 0)
                    round_probs(n, s)

            iteration(0, 0, True, True, first=True)
            iteration(1, 1, True, True)
            with act.Fori(1, NPAIR // 2 - 1) as m:
                iteration(2 * m, 0, True, True)
                iteration(2 * m + 1, 1, True, True)
            iteration(NPAIR - 2, 0, True, False)
            iteration(NPAIR - 1, 1, False, False)
            evac_o(NPAIR - 1, 1)

        @block.vector
        def _(dve):
            def stats(t, slot):
                wait(dve, tile_loaded[slot], 2 * DMA * (t // 2 + 1))
                wait(dve, aggregated, 2 * t)
                dve.bn_stats(bn_c[:], ctx_raw[slot][:]).then_inc(bn_done, 1)
                dve.bn_stats(bn_x[:], x_raw[slot][:]).then_inc(bn_done, 1)
                dve.wait_ge(bn_done, 2 * t + 2)
                dve.tensor_copy(carry_dve[:], bn_c[:, 0:1])
                dve.bn_aggr(mv_c[slot][:], bn_c[:]).then_inc(aggregated, 1)
                dve.bn_aggr(mv_x[slot][:], bn_x[:]).then_inc(aggregated, 1)
                dve.wait_ge(aggregated, 2 * t + 2)
                dve.tensor_scalar(var_sb[slot][:, 0:1], mv_c[slot][:, 1:2], EPS, None, ALU.add).then_inc(stats_ready, 1)
                dve.tensor_scalar(var_sb[slot][0:64, 1:2], mv_x[slot][:, 1:2], 1.0 + EPS, EPS * EPS,
                                  ALU.mult, ALU.add).then_inc(stats_ready, 1)

            def normalize(t, slot):
                wait(dve, rstd_ready, t + 1)
                wait(dve, turned, t)
                dve.tensor_scalar(ctx_n[:], ctx_raw[slot][:], mv_c[slot][:, 0:1], rstd_sb[slot][:, 0:1],
                                  ALU.subtract, ALU.mult).then_inc(normed, 1)
                dve.tensor_scalar(x_n[:], x_raw[slot][:], mv_x[slot][:, 0:1], rstd_sb[slot][0:64, 1:2],
                                  ALU.subtract, ALU.mult).then_inc(normed, 1)

            def split_tile(t):
                dve.wait_ge(affine_done, 4 * t + 4)
                bp, cs = t // STEPS, t % STEPS
                c_at, x_at = slice(cs * P, cs * P + P), slice(cs * 64, cs * 64 + 64)
                dve.tensor_copy(ctxT_hi[:, bp, :, c_at], ctx_t32[:]).then_inc(tile_hi, 1)
                dve.tensor_copy(xT_hi[:, bp, :, x_at], x_t32[:]).then_inc(tile_hi, 1)
                dve.wait_ge(tile_hi, 2 * t + 2)
                dve.tensor_tensor(ctxT_lo[:, bp, :, c_at], ctx_t32[:], ctxT_hi[:, bp, :, c_at],
                                  ALU.subtract).then_inc(tile_split, 1)
                dve.tensor_tensor(xT_lo[:, bp, :, x_at], x_t32[:], xT_hi[:, bp, :, x_at],
                                  ALU.subtract).then_inc(tile_split, 1)

            def split_weights(w, par):
                dve.wait_ge(w_hi_done, w + 1)
                dve.tensor_tensor(w_lo[par][:], w_raw[:], w_hi[par][:], ALU.subtract).then_inc(w_split, 1)

            def split_q(p):
                wait(dve, q_hi_done, p + 1)
                for h in range(2):
                    wait(dve, q_stacked[h], 4 * DMA * p)
                dve.tensor_tensor(q_lo[:], job_ps[0][:], q_hi[:], ALU.subtract).then_inc(q_split, 1)

            def rope_times(p):
                wait(dve, k_evac, 2 * p + 2)
                wait(dve, k_swapped, 4 * DMA * (p + 1))
                dve.tensor_tensor(k32[:], k32[:], cos_sb[:], ALU.mult).then_inc(k_times, 1)
                dve.tensor_tensor(k_swap[:], k_swap[:], sin_sb[:], ALU.mult).then_inc(k_times, 1)

            def rope_add(p):
                wait(dve, k_times, 2 * p + 2)
                dve.tensor_tensor(k32[:], k32[:], k_swap[:], ALU.add).then_inc(k_roped, 1)

            def split_k(p, par):
                for h in range(2):
                    wait(dve, k_hi_done, 2 * p + 1 + h)
                    rows = slice(DH * h, DH * h + DH)
                    other = slice(DH * (1 - h), DH * (1 - h) + DH)
                    dve.tensor_tensor(k_stack[par][h][other, :], k32[rows, :], k_stack[par][h][rows, :],
                                      ALU.subtract).then_inc(k_split, 1)

            def split_v(p, par, half):
                wait(dve, v_hi_done, 2 * p + 1 + half)
                tiles = slice(4 * half, 4 * half + 4)
                dve.tensor_tensor(v_part(v_lo[par], tiles), job_ps[half][:].rearrange("p (t a d) -> p t a d", t=4, a=2),
                                  v_part(v_hi[par], tiles), ALU.subtract).then_inc(v_split, 1)

            def split_probs(n, s):
                wait(dve, p_hi_done, STEPS * n + s + 1)
                dve.tensor_tensor(p_lo[s % 2][:], probs[s % 2][:], p_hi[s % 2][:],
                                  ALU.subtract).then_inc(p_split_dve, 1)

            def clip(n, s):
                g = STEPS * n + s
                wait(dve, exp_done, g + 1)
                dve.tensor_scalar(probs[s % 2][:], probs[s % 2][:], CLIP_HI, CLIP_LO,
                                  ALU.min, ALU.max).then_inc(clipped, 1)

            def invert(n, half):
                for h in range(2):
                    wait(dve, o_evac[h], 2 * n + 2)
                part = den[:, 256 * half:256 * half + 256]
                dve.reciprocal(part, part).then_inc(den_inv, 1)

            def split_o(n):
                wait(dve, den_inv, 2 * n + 2)
                dve.tensor_tensor(o_raw[:], o_raw[:], den[:], ALU.mult).then_inc(o_scaled, 1)
                wait(dve, o_scaled, n + 1)
                wait(dve, y_projected, 2 * n)
                dve.tensor_copy(o_hi[:], o_raw[:]).then_inc(o_hi_done, 1)
                wait(dve, o_hi_done, n + 1)
                dve.tensor_tensor(o_lo[:], o_raw[:], o_hi[:], ALU.subtract).then_inc(o_split, 1)

            def add_y(n, part):
                for mt in range(2):
                    wait(dve, y_projected, 2 * n + 1 + mt)
                    wait(dve, y_added, 2 * n - 1 + mt)
                    acc = yT[:, mt, bass.ds((n // PAIRS) * NQ, NQ)]
                    dve.tensor_tensor(acc, job_ps[mt][:], acc, ALU.add).then_inc(y_added, 1)

            dve.wait_ge(power_ready, 3)
            stats(0, 0)
            split_weights(0, 0)
            for t in range(FIRST_TILES):
                if t + 1 < FIRST_TILES:
                    stats(t + 1, (t + 1) % 2)
                normalize(t, t % 2)
                if t == 3:
                    split_weights(1, 1)
                if t:
                    split_tile(t - 1)
            split_tile(FIRST_TILES - 1)
            dve.wait_ge(consts_loaded, 9 * DMA)
            for q in (0, 2):
                rows = slice(32 * q, 32 * q + 32)
                dve.tensor_scalar(sin_sb[rows, :], sin_sb[rows, :], -1.0, None, ALU.mult).then_inc(sin_signed, 1)
            dve.wait_ge(sin_signed, 2)
            split_q(0)
            rope_times(0)
            rope_add(0)
            split_v(0, 0, 0)
            split_v(0, 0, 1)
            split_k(0, 0)
            dve.wait_ge(y_zeroed, 1)
            for mt in range(2):
                dve.tensor_scalar(yT[:, mt, :], yT[:, mt, :], bo[:, mt:mt + 1], None, ALU.add).then_inc(y_biased, 1)
            dve.wait_ge(y_biased, 2)

            def iteration(n, par, project, prep, first=False):
                for s in range(STEPS):
                    clip(n, s)
                    if s == 0 and prep:
                        stats(n + FIRST_TILES, 1 - par)
                    if s == 1 and prep:
                        normalize(n + FIRST_TILES, 1 - par)
                    if s == 2 and project:
                        split_q(n + 1)
                    if s in (2, 3) and not first:
                        invert(n - 1, s - 2)
                    if s == 4 and project:
                        rope_times(n + 1)
                    if s == 4 and project:
                        rope_add(n + 1)
                    if s == 5 and not first:
                        split_o(n - 1)
                    if s in (5, 6) and project:
                        split_v(n + 1, 1 - par, s - 5)
                    if s == 6 and project:
                        split_k(n + 1, 1 - par)
                    if s == 7 and not first:
                        add_y(n - 1, par)
                    if s in DVE_STEPS:
                        split_probs(n, s)

            iteration(0, 0, True, True, first=True)
            iteration(1, 1, True, True)
            with dve.Fori(1, NPAIR // 2 - 1) as m:
                iteration(2 * m, 0, True, True)
                iteration(2 * m + 1, 1, True, True)
            iteration(NPAIR - 2, 0, True, False)
            iteration(NPAIR - 1, 1, False, False)
            invert(NPAIR - 1, 0)
            invert(NPAIR - 1, 1)
            split_o(NPAIR - 1)
            add_y(NPAIR - 1, 1)


def ffn_phase(nc, x, selT, keys, values, sel_dram, out, yT):
    with ExitStack() as st:
        def sb(name, shape, dt=F32):
            return st.enter_context(nc.sbuf_tensor(name, shape, dt))

        def psum(name, shape):
            return st.enter_context(nc.psum_tensor(name, shape, F32))

        def sem(name):
            return st.enter_context(nc.semaphore(name))

        TILES = ALL // P
        PER = TILES // CHUNKS
        ARING = 4
        FLAG = 3
        GROUP = 4
        GROUPS = EXPERTS // GROUP

        ident = sb("ident2", [P, P])
        x2 = sb("x2", [P, TILES, D])
        sel_w = sb("sel_w", [P, KT, EXPERTS])
        sel_hi = sb("sel_hi", [P, KT, P], F32R)
        sel_lo = sb("sel_lo", [P, KT, P], F32R)
        w_raw = sb("w_raw2", [P, 2048])
        key_hi = sb("key_hi", [P, KT, EXPERTS * HID], F32R)
        key_lo = sb("key_lo", [P, KT, EXPERTS * HID], F32R)
        val_hi = sb("val_hi", [P, EXPERTS, D], F32R)
        val_lo = sb("val_lo", [P, EXPERTS, D], F32R)
        bn = sb("bn2", [P, 6])
        mv = [sb(f"mv2{i}", [P, 2]) for i in range(2)]
        rstd = [sb(f"rstd2{i}", [P, 2]) for i in range(2)]
        power = sb("power2", [P, 1])
        x_n = [sb(f"x_n2{i}", [P, D]) for i in range(2)]
        xT_hi = sb("x2T_hi", [P, KT, ALL], F32R)
        xT_lo = sb("x2T_lo", [P, KT, ALL], F32R)
        gate = [sb(f"gate{i}", [EXPERTS, 512]) for i in range(CHUNKS)]
        sel_all = [sb(f"sel_all{i}", [P, GROUP * 512]) for i in range(2)]
        act32 = [sb(f"act32{i}", [P, 512]) for i in range(ARING)]
        act_hi = [sb(f"act_hi{i}", [P, 512], F32R) for i in range(ARING)]
        act_lo = [sb(f"act_lo{i}", [P, 512], F32R) for i in range(ARING)]
        outT = sb("outT", [P, 2, 512])
        x_out = [sb(f"x_out{i}", [P, 2, D]) for i in range(2)]

        h_ps = [psum(f"h_ps{i}", [P, 512]) for i in range(ARING)]
        out_ps = [psum(f"out_ps{i}", [P, 512]) for i in range(2)]
        fin_ps = [psum(f"fin_ps{i}", [P, 2, D]) for i in range(2)]

        ident_zero = sem("ident_zero2")
        ident_ready = sem("ident_ready2")
        sel_zero = sem("sel_zero")
        x_loaded = sem("x_loaded")
        sel_w_loaded = sem("sel_w_loaded")
        raw_loaded = sem("raw_loaded")
        sel_hi_done = sem("sel_hi_done")
        sel_split = sem("sel_split")
        w_hi_done = sem("w_hi_done2")
        w_split = sem("w_split2")
        y_turned = sem("y_turned")
        fin_added = sem("fin_added")
        bn_done = sem("bn_done2")
        stats_ready = sem("stats_ready2")
        power_ready = sem("power_ready2")
        eps_added = sem("eps_added")
        rstd_ready = sem("rstd_ready2")
        normed = sem("normed2")
        x_turned = sem("x_turned")
        x_hi_done = sem("x_hi_done")
        x_split = sem("x_split")
        logits_ready = sem("logits_ready")
        gate_exp = sem("gate_exp")
        gate_plus = sem("gate_plus")
        gate_ready = sem("gate_ready")
        stored = sem("stored")
        sel_loaded = [sem(f"sel_loaded{i}") for i in range(2)]
        h_ready = sem("h_ready")
        gated = sem("gated")
        act_hi_done = sem("act_hi_done")
        act_split = sem("act_split")
        summed = sem("summed")
        out_evac = sem("out_evac")
        out_turned = sem("out_turned")

        lots = [(key_hi[:, k, :], key_lo[:, k, :]) for k in range(KT)]
        lots += [(val_hi[:, 8 * i:8 * i + 8, :].rearrange("p e d -> p (e d)"),
                  val_lo[:, 8 * i:8 * i + 8, :].rearrange("p e d -> p (e d)")) for i in range(2)]

        block = st.enter_context(nc.Block())

        @block.sync
        def _(sp):
            for q in range(4):
                sp.dma_start(x2[:, 4 * q:4 * q + 4, :],
                             x[4 * q * P:(4 * q + 4) * P, :].rearrange("(t p) d -> p t d", p=P)).then_inc(x_loaded, DMA)
                if q == 0:
                    for k in range(KT):
                        sp.dma_start(sel_w[:, k, :], selT[k * P:(k + 1) * P, :]).then_inc(sel_w_loaded, DMA)
            for lot in range(4):
                wait(sp, w_split, lot)
                if lot < 2:
                    sp.dma_start(w_raw[:].rearrange("p (e h) -> p e h", h=HID),
                                 keys[:, lot * P:(lot + 1) * P, :].rearrange("e d h -> d e h")).then_inc(raw_loaded, DMA)
                else:
                    e = 8 * (lot - 2)
                    sp.dma_start(w_raw[:].rearrange("p (e d) -> p e d", d=D),
                                 values[e:e + 8, :, :].rearrange("e h d -> h e d")).then_inc(raw_loaded, DMA)
            for c in range(CHUNKS):
                sp.wait_ge(gate_ready, c + 1)
                sp.dma_start(sel_dram[c, :, :], gate[c][:]).then_inc(stored, DMA)
            sp.wait_ge(stored, DMA * CHUNKS)

            def load_gates(c, q, slot):
                wait(sp, gated, GROUP * (GROUPS * c + q - 1))
                src = sel_dram[bass.ds(c, 1), GROUP * q:GROUP * q + GROUP, :].rearrange("a e n -> a (e n)")
                sp.dma_start(sel_all[slot][:], src[0, :].partition_broadcast(P)).then_inc(sel_loaded[slot], DMA)

            def store(c):
                for i in range(2):
                    sp.wait_ge(fin_added, TILES + 2 * c + i + 1)
                    sp.dma_start(out[bass.ds(c * 512 + i * 256, 256), :].rearrange("(t p) d -> p t d", p=P),
                                 x_out[i][:]).then_inc(stored, DMA)

            load_gates(0, 0, 0)
            load_gates(0, 1, 1)

            def chunk(c, first=False, last=False):
                load_gates(c, 2, 0)
                load_gates(c, 3, 1)
                if not first:
                    store(c - 1)
                if not last:
                    load_gates(c + 1, 0, 0)
                    load_gates(c + 1, 1, 1)

            chunk(0, first=True)
            with sp.Fori(1, CHUNKS - 1) as c:
                chunk(c)
            chunk(CHUNKS - 1, last=True)
            store(CHUNKS - 1)
            sp.wait_ge(stored, DMA * 3 * CHUNKS)

        @block.gpsimd
        def _(pool):
            pool.memset(ident[:], 0.0).then_inc(ident_zero, 1)
            pool.wait_ge(ident_zero, 1)
            pool.affine_select(out=ident[:], in_=ident[:], compare_op=ALU.not_equal, fill=1.0, base=0,
                               pattern=[[-1, P]], channel_multiplier=1).then_inc(ident_ready, 1)
            pool.memset(power[:], -0.5).then_inc(power_ready, 1)
            pool.wait_ge(power_ready, 1)
            for t in range(TILES):
                pool.wait_ge(stats_ready, t + 1)
                wait(pool, normed, t - 1)
                pool.tensor_scalar(rstd[t % 2][:, 0:1], mv[t % 2][:, 1:2], EPS, None, ALU.add).then_inc(eps_added, 1)
                pool.wait_ge(eps_added, t + 1)
                pool.tensor_tensor(rstd[t % 2][:, 1:2], rstd[t % 2][:, 0:1], power[:], ALU.pow).then_inc(rstd_ready, 1)

            def split_act(g, e):
                wait(pool, act_hi_done, g + 1)
                pool.tensor_tensor(act_lo[e % ARING][:], act32[e % ARING][:], act_hi[e % ARING][:],
                                   ALU.subtract).then_inc(act_split, 1)

            with pool.Fori(0, CHUNKS) as c:
                for e in range(EXPERTS):
                    split_act(EXPERTS * c + e, e)

        @block.tensor
        def _(pe):
            def product(out_, terms, start=True, stop=True):
                for i, (lhsT, rhs) in enumerate(terms):
                    mm = pe.matmul(out_, lhsT, rhs, start=start and i == 0, stop=stop and i == len(terms) - 1)
                return mm

            def turn_y(t):
                wait(pe, fin_added, t - 1)
                for mt in range(2):
                    tr = pe.transpose(fin_ps[t % 2][:, 0, mt * P:(mt + 1) * P], yT[:, mt, t * P:(t + 1) * P], ident[:])
                tr.then_inc(y_turned, 1)

            def turn_x(t):
                pe.wait_ge(normed, t + 1)
                wait(pe, x_split, t - 1)
                for k in range(KT):
                    tr = pe.transpose(h_ps[t % 2][:, k * P:(k + 1) * P], x_n[t % 2][:, k * P:(k + 1) * P], ident[:])
                tr.then_inc(x_turned, 1)

            def logits(c):
                pe.wait_ge(x_split, PER * (c + 1))
                pe.wait_ge(sel_split, 2)
                wait(pe, gate_exp, c - 1)
                cols_ = slice(c * 512, (c + 1) * 512)
                terms = []
                for k in range(KT):
                    terms += [(sel_hi[:, k, :], xT_hi[:, k, cols_]), (sel_hi[:, k, :], xT_lo[:, k, cols_]),
                              (sel_lo[:, k, :], xT_hi[:, k, cols_])]
                product(h_ps[2 + c % 2][:], terms).then_inc(logits_ready, 1)

            pe.wait_ge(ident_ready, 1)
            turn_y(0)
            for t in range(TILES):
                if t + 1 < TILES:
                    turn_y(t + 1)
                turn_x(t)
                if t % PER == 0 and t:
                    logits(t // PER - 1)
            logits(CHUNKS - 1)
            pe.wait_ge(x_split, TILES)
            pe.wait_ge(gate_exp, CHUNKS)
            pe.wait_ge(w_split, 4)

            def expert_in(c, g, e):
                wait(pe, gated, g - ARING + 1)
                cols_ = bass.ds(c * 512, 512)
                terms = []
                for k in range(KT):
                    hi, lo = key_hi[:, k, e * HID:(e + 1) * HID], key_lo[:, k, e * HID:(e + 1) * HID]
                    terms += [(hi, xT_hi[:, k, cols_]), (hi, xT_lo[:, k, cols_]), (lo, xT_hi[:, k, cols_])]
                product(h_ps[e % ARING][:], terms).then_inc(h_ready, 1)

            def expert_out(c, g, e):
                pe.wait_ge(act_split, g + 1)
                for mt in range(2):
                    if e == 0:
                        wait(pe, out_evac, 2 * (c - 1) + 1 + mt)
                    hi, lo = val_hi[:, e, mt * P:(mt + 1) * P], val_lo[:, e, mt * P:(mt + 1) * P]
                    mm = product(out_ps[mt][:], [(hi, act_hi[e % ARING][:]), (hi, act_lo[e % ARING][:]),
                                                 (lo, act_hi[e % ARING][:])],
                                 start=(e == 0), stop=(e == EXPERTS - 1))
                mm.then_inc(summed, 1)

            def turn_out(c):
                pe.wait_ge(out_evac, 2 * c + 2)
                for i in range(2):
                    wait(pe, fin_added, TILES + 2 * (c - 1) + 1 + i)
                    for j in range(2):
                        for mt in range(2):
                            at = (2 * i + j) * P
                            tr = pe.transpose(fin_ps[i][:, j, mt * P:(mt + 1) * P], outT[:, mt, at:at + P], ident[:])
                    tr.then_inc(out_turned, 1)

            pe.wait_ge(fin_added, TILES)

            def chunk(c, first=False):
                for e in range(EXPERTS):
                    g = EXPERTS * c + e
                    expert_in(c, g, e)
                    if e >= FLAG:
                        expert_out(c, g - FLAG, e - FLAG)
                    elif not first:
                        expert_out(c - 1, g - FLAG, e - FLAG + EXPERTS)
                    if e == 5 and not first:
                        turn_out(c - 1)

            chunk(0, first=True)
            with pe.Fori(1, CHUNKS) as c:
                chunk(c)
            for e in range(EXPERTS - FLAG, EXPERTS):
                expert_out(CHUNKS - 1, EXPERTS * (CHUNKS - 1) + e, e)
            turn_out(CHUNKS - 1)

        @block.scalar
        def _(act):
            def round_x(t):
                act.wait_ge(x_turned, t + 1)
                dst = xT_hi[:, :, t * P:(t + 1) * P]
                act.copy(dst, h_ps[t % 2][:, 0:KT * P].rearrange("p (k n) -> p k n", k=KT)).then_inc(x_hi_done, 1)

            def exp_gate(c):
                act.wait_ge(logits_ready, c + 1)
                act.activation(gate[c][:], h_ps[2 + c % 2][0:EXPERTS, :], ACT.Exp, scale=-1.0).then_inc(gate_exp, 1)

            def round_weights(lot):
                act.wait_ge(raw_loaded, DMA * (lot + 1))
                act.copy(lots[lot][0], w_raw[:]).then_inc(w_hi_done, 1)

            for t in range(TILES):
                round_x(t)
                if t % PER == 0 and t:
                    round_weights(t // PER - 1)
                    if t // PER >= 2:
                        exp_gate(t // PER - 2)
            round_weights(3)
            exp_gate(CHUNKS - 2)
            exp_gate(CHUNKS - 1)

            def round_act(g, e):
                act.wait_ge(gated, g + 1)
                wait(act, summed, g - ARING + 1)
                act.copy(act_hi[e % ARING][:], act32[e % ARING][:]).then_inc(act_hi_done, 1)

            def evac_out(c):
                act.wait_ge(summed, EXPERTS * (c + 1))
                for mt in range(2):
                    act.copy(outT[:, mt, :], out_ps[mt][:]).then_inc(out_evac, 1)

            def chunk(c, first=False):
                for e in range(EXPERTS):
                    if e == FLAG and not first:
                        evac_out(c - 1)
                    round_act(EXPERTS * c + e, e)

            chunk(0, first=True)
            with act.Fori(1, CHUNKS) as c:
                chunk(c)
            evac_out(CHUNKS - 1)

        @block.vector
        def _(dve):
            def residual(t):
                dve.wait_ge(y_turned, t + 1)
                if t % 4 == 0:
                    dve.wait_ge(x_loaded, DMA * 4)
                dve.tensor_tensor(x2[:, t, :], fin_ps[t % 2][:, 0, :], x2[:, t, :], ALU.add).then_inc(fin_added, 1)
                dve.wait_ge(fin_added, t + 1)
                wait(dve, stats_ready, t)
                dve.bn_stats(bn[:], x2[:, t, :]).then_inc(bn_done, 1)
                dve.wait_ge(bn_done, t + 1)
                dve.bn_aggr(mv[t % 2][:], bn[:]).then_inc(stats_ready, 1)

            def normalize(t):
                dve.wait_ge(rstd_ready, t + 1)
                wait(dve, x_turned, t - 1)
                dve.tensor_scalar(x_n[t % 2][:], x2[:, t, :], mv[t % 2][:, 0:1], rstd[t % 2][:, 1:2],
                                  ALU.subtract, ALU.mult).then_inc(normed, 1)

            def split_x(t):
                dve.wait_ge(x_hi_done, t + 1)
                dve.tensor_tensor(xT_lo[:, :, t * P:(t + 1) * P],
                                  h_ps[t % 2][:, 0:KT * P].rearrange("p (k n) -> p k n", k=KT),
                                  xT_hi[:, :, t * P:(t + 1) * P], ALU.subtract).then_inc(x_split, 1)

            def split_weights(lot):
                dve.wait_ge(w_hi_done, lot + 1)
                dve.tensor_tensor(lots[lot][1], w_raw[:], lots[lot][0], ALU.subtract).then_inc(w_split, 1)

            def invert_gate(c):
                dve.wait_ge(gate_exp, c + 1)
                dve.tensor_scalar(gate[c][:], gate[c][:], 1.0, None, ALU.add).then_inc(gate_plus, 1)
                dve.wait_ge(gate_plus, c + 1)
                dve.reciprocal(gate[c][:], gate[c][:]).then_inc(gate_ready, 1)

            dve.memset(raw(sel_hi), 0.0).then_inc(sel_zero, 1)
            dve.memset(raw(sel_lo), 0.0).then_inc(sel_zero, 1)
            dve.wait_ge(sel_zero, 2)
            dve.wait_ge(sel_w_loaded, 2 * DMA)
            dve.tensor_copy(sel_hi[:, :, 0:EXPERTS], sel_w[:]).then_inc(sel_hi_done, 1)
            dve.wait_ge(sel_hi_done, 1)
            dve.tensor_tensor(sel_lo[:, :, 0:EXPERTS], sel_w[:], sel_hi[:, :, 0:EXPERTS],
                              ALU.subtract).then_inc(sel_split, 2)
            residual(0)
            for t in range(TILES):
                if t + 1 < TILES:
                    residual(t + 1)
                normalize(t)
                if t:
                    split_x(t - 1)
                    if t % PER == 0:
                        if t // PER >= 2:
                            split_weights(t // PER - 2)
                        if t // PER >= 3:
                            invert_gate(t // PER - 3)
            split_x(TILES - 1)
            split_weights(2)
            split_weights(3)
            for c in range(1, CHUNKS):
                invert_gate(c)

            def gate_h(c, e):
                g = EXPERTS * c + e
                dve.wait_ge(h_ready, g + 1)
                q = e // GROUP
                if e % GROUP == 0:
                    wait(dve, sel_loaded[q % 2], DMA * (2 * c + q // 2 + 1))
                wait(dve, act_split, g - ARING + 1)
                at = (e % GROUP) * 512
                dve.scalar_tensor_tensor(out=act32[e % ARING][:], in0=h_ps[e % ARING][:], scalar=0.0,
                                         in1=sel_all[q % 2][:, at:at + 512], op0=ALU.max, op1=ALU.mult
                                         ).then_inc(gated, 1)

            def add_out(c):
                for i in range(2):
                    dve.wait_ge(out_turned, 2 * c + i + 1)
                    dve.wait_ge(stored, DMA * (CHUNKS + 2 * c))
                    dve.tensor_tensor(x_out[i][:], fin_ps[i][:], x2[:, bass.ds(c * PER + 2 * i, 2), :],
                                      ALU.add).then_inc(fin_added, 1)

            def chunk(c, first=False):
                for e in range(EXPERTS):
                    gate_h(c, e)
                    if e == 6 and not first:
                        add_out(c - 1)

            chunk(0, first=True)
            with dve.Fori(1, CHUNKS) as c:
                chunk(c)
            add_out(CHUNKS - 1)


def build(nc, x, ctx_in, cosT, sinT, cols, Wq, Wkv, Wo, selT, keys, values, out, sel_dram):
    with ExitStack() as st:
        yT = st.enter_context(nc.sbuf_tensor("yT", [P, 2, ALL], F32))
        attention_phase(nc, x, ctx_in, cosT, sinT, cols, Wq, Wkv, Wo, yT)
        ffn_phase(nc, x, selT, keys, values, sel_dram, out, yT)


def kernel(x, ctx_1024, L0_xattn_cos, L0_xattn_sin, L0_xattn_ln_lat_g, L0_xattn_ln_lat_b, L0_xattn_ln_ctx_g,
           L0_xattn_ln_ctx_b, L0_xattn_Wq, L0_xattn_Wkv, L0_xattn_Wo, L0_xattn_bo, L0_ffn_expert_sel,
           L0_ffn_keys, L0_ffn_values):
    import numpy as np
    import concourse.bacc as bacc
    from concourse.bass_utils import run_bass_kernel_spmd

    vectors = [L0_xattn_ln_lat_g, L0_xattn_ln_lat_b, L0_xattn_ln_ctx_g, L0_xattn_ln_ctx_b, L0_xattn_bo]
    cols = np.concatenate([np.asarray(v).reshape(KT, P) for v in vectors], axis=0).T
    arrays = {
        "x": np.asarray(x).reshape(ALL, D),
        "ctx": np.asarray(ctx_1024).reshape(B * S, D),
        "cosT": np.asarray(L0_xattn_cos).T,
        "sinT": np.asarray(L0_xattn_sin).T,
        "cols": cols,
        "Wq": L0_xattn_Wq,
        "Wkv": L0_xattn_Wkv,
        "Wo": L0_xattn_Wo,
        "selT": np.asarray(L0_ffn_expert_sel).T,
        "keys": L0_ffn_keys,
        "values": L0_ffn_values,
    }
    arrays = {name: np.ascontiguousarray(a) for name, a in arrays.items()}
    nc = bacc.Bacc("TRN2", target_bir_lowering=False, num_devices=1)
    ins = [nc.dram_tensor(name, a.shape, mybir.dt.from_np(a.dtype), kind="ExternalInput").ap()
           for name, a in arrays.items()]
    out = nc.dram_tensor("out", (ALL, D), F32, kind="ExternalOutput").ap()
    sel_dram = nc.dram_tensor("sel_dram", (CHUNKS, EXPERTS, 512), F32, kind="Internal").ap()
    build(nc, *ins, out, sel_dram)
    r = run_bass_kernel_spmd(nc, [arrays], core_ids=[0])
    return r.results[0]["out"].reshape(B, NQ, D)
```

```python
from contextlib import ExitStack

import concourse.bass as bass
from concourse import mybir

F32 = mybir.dt.float32
F32R = mybir.dt.float32r
ALU = mybir.AluOpType
ACT = mybir.ActivationFunctionType

P = 128
DMA = 16
B, NQ, D = 4, 512, 256
S = 1024
HEADS, DH = 16, 64
INNER = HEADS * DH
KT = D // P
PAIRS = HEADS // 2
NPAIR = B * PAIRS
STEPS = 8
ALL = B * NQ
EXPERTS, HID = 16, 128
CHUNKS = ALL // 512
PER = 512 // P
WC = 3 * KT * P + D
EPS = 1e-5
CLIP_HI = 59874.141715197816
CLIP_LO = 1.670170079024566e-05
FIRST_TILES = 10
LAG = 2
POOL_STEPS = (2, 4, 6)
DVE_STEPS = (0, 1, 3, 5, 7)


def wait(eng, sem, value):
    if isinstance(value, int) and value <= 0:
        return
    eng.wait_ge(sem, value)


def raw(t):
    return t[:].bitcast(F32)


class Shared:
    pass


def shared_state(nc, st):
    def sb(name, shape, dt=F32):
        return st.enter_context(nc.sbuf_tensor(name, shape, dt))

    def sem(name):
        return st.enter_context(nc.semaphore(name))

    sh = Shared()
    sh.yT = sb("yT", [P, 2, ALL])
    sh.ident = sb("ident", [P, P])
    sh.x2_head = sb("x2_head", [P, PER, D])
    sh.xT_hi = sb("xT_hi", [P, 2, KT, NQ], F32R)
    sh.xT_lo = sb("xT_lo", [P, 2, KT, NQ], F32R)
    sh.wide_hi = sb("wide_hi", [P, 2, KT, S], F32R)
    sh.wide_lo = sb("wide_lo", [P, 2, KT, S], F32R)
    sh.sel_w = sb("sel_w", [P, KT, EXPERTS])
    sh.sel_hi = sb("sel_hi", [P, KT, P], F32R)
    sh.sel_lo = sb("sel_lo", [P, KT, P], F32R)
    sh.gate = sb("gate", [EXPERTS, 512])
    sh.o_raw = sb("o_raw", [P, NQ])
    sh.den = sb("den", [P, NQ])
    sh.o_hi = sb("o_hi", [P, NQ], F32R)
    sh.o_lo = sb("o_lo", [P, NQ], F32R)
    sh.w_hi1 = sb("w_hi1", [P, WC], F32R)
    sh.w_lo1 = sb("w_lo1", [P, WC], F32R)
    sh.k32 = sb("k32", [P, S])
    sh.w_raw = sb("w_raw", [P, WC])
    sh.job_ps = [st.enter_context(nc.psum_tensor(f"job_ps{i}", [P, 512], F32)) for i in range(2)]
    sh.o_evac = [sem("o_evac_a"), sem("o_evac_b")]
    sh.ident_ready = sem("ident_ready")
    sh.den_inv = sem("den_inv")
    sh.o_scaled = sem("o_scaled")
    sh.o_hi_done = sem("o_hi_done")
    sh.o_split = sem("o_split")
    sh.w_split = sem("w_split")
    sh.y_projected = sem("y_projected")
    sh.y_added = sem("y_added")
    sh.logits_ready = sem("logits_ready")
    sh.gate_exp = sem("gate_exp")
    sh.gate_plus = sem("gate_plus")
    sh.gate_ready = sem("gate_ready")
    sh.gate_stored = sem("gate_stored")
    sh.key_split = sem("key_split")
    sh.first_gates = sem("first_gates")
    sh.first_values = sem("first_values")
    return sh


def product(pe, out, terms, start=True, stop=True):
    for i, (lhsT, rhs) in enumerate(terms):
        mm = pe.matmul(out, lhsT, rhs, start=start and i == 0, stop=stop and i == len(terms) - 1)
    return mm


def project_y(pe, sh, n, mt, w_hi, w_lo):
    if mt == 0:
        wait(pe, sh.o_split, n + 1)
        if isinstance(n, int) and n >= NPAIR - 3:
            wait(pe, sh.w_split, n + 3)
    at = 3 * KT * P + mt * P
    hi, lo = w_hi[:, at:at + P], w_lo[:, at:at + P]
    product(pe, sh.job_ps[mt][:], [(hi, sh.o_hi[:]), (hi, sh.o_lo[:]), (lo, sh.o_hi[:])]).then_inc(sh.y_projected, 1)


def invert_den(dve, sh, n, half):
    for h in range(2):
        wait(dve, sh.o_evac[h], 2 * n + 2)
    part = sh.den[:, 256 * half:256 * half + 256]
    dve.reciprocal(part, part).then_inc(sh.den_inv, 1)


def split_o(dve, sh, n):
    wait(dve, sh.den_inv, 2 * n + 2)
    dve.tensor_tensor(sh.o_raw[:], sh.o_raw[:], sh.den[:], ALU.mult).then_inc(sh.o_scaled, 1)
    wait(dve, sh.o_scaled, n + 1)
    wait(dve, sh.y_projected, 2 * n)
    dve.tensor_copy(sh.o_hi[:], sh.o_raw[:]).then_inc(sh.o_hi_done, 1)
    wait(dve, sh.o_hi_done, n + 1)
    dve.tensor_tensor(sh.o_lo[:], sh.o_raw[:], sh.o_hi[:], ALU.subtract).then_inc(sh.o_split, 1)


def add_y(dve, sh, n, mt):
    wait(dve, sh.y_projected, 2 * n + 1 + mt)
    wait(dve, sh.y_added, 2 * n - 1 + mt)
    acc = sh.yT[:, mt, bass.ds((n // PAIRS) * NQ, NQ)]
    dve.tensor_tensor(acc, sh.job_ps[mt][:], acc, ALU.add).then_inc(sh.y_added, 1)


def logits(pe, sh, rhs_hi, rhs_lo):
    terms = []
    for k in range(KT):
        terms += [(sh.sel_hi[:, k, :], rhs_hi(k)), (sh.sel_hi[:, k, :], rhs_lo(k)), (sh.sel_lo[:, k, :], rhs_hi(k))]
    product(pe, sh.job_ps[0][:], terms).then_inc(sh.logits_ready, 1)


def exp_gate(act, sh, c):
    wait(act, sh.logits_ready, c + 1)
    wait(act, sh.gate_stored, DMA * c)
    act.activation(sh.gate[:], sh.job_ps[0][0:EXPERTS, :], ACT.Exp, scale=-1.0).then_inc(sh.gate_exp, 1)


def invert_gate(dve, sh, c, half):
    if half == 0:
        wait(dve, sh.gate_exp, c + 1)
        dve.tensor_scalar(sh.gate[:], sh.gate[:], 1.0, None, ALU.add).then_inc(sh.gate_plus, 1)
        wait(dve, sh.gate_plus, c + 1)
    part = sh.gate[:, 256 * half:256 * half + 256]
    dve.reciprocal(part, part).then_inc(sh.gate_ready, 1)


def store_gates(sp, sh, sel_dram, c):
    wait(sp, sh.gate_ready, 2 * c + 2)
    dst = sel_dram[bass.ds(c, 1), :, :].rearrange("a e n -> (a e) n")
    sp.dma_start(dst, sh.gate[:]).then_inc(sh.gate_stored, DMA)


def attention_phase(nc, sh, x, ctx_in, cosT, sinT, cols, Wq, Wkv, Wo, selT, keys, values, sel_dram):
    with ExitStack() as st:
        def sb(name, shape, dt=F32):
            return st.enter_context(nc.sbuf_tensor(name, shape, dt))

        def psum(name, shape):
            return st.enter_context(nc.psum_tensor(name, shape, F32))

        def sem(name):
            return st.enter_context(nc.semaphore(name))

        yT, ident, job_ps, x2_head = sh.yT, sh.ident, sh.job_ps, sh.x2_head
        xT_hi, xT_lo, ctxT_hi, ctxT_lo = sh.xT_hi, sh.xT_lo, sh.wide_hi, sh.wide_lo
        o_raw, den, k32, w_raw = sh.o_raw, sh.den, sh.k32, sh.w_raw
        ident_ready, o_evac, o_split, w_split = sh.ident_ready, sh.o_evac, sh.o_split, sh.w_split
        y_projected, y_added = sh.y_projected, sh.y_added

        cos_sb = sb("cos_sb", [P, S])
        sin_sb = sb("sin_sb", [P, S])
        col_sb = sb("col_sb", [P, 10])
        ctx_raw = [sb(f"ctx_raw{i}", [P, D]) for i in range(2)]
        x_raw = [sb(f"x_raw{i}", [64, D]) for i in range(2)]
        bn_c = sb("bn_c", [P, 6])
        bn_x = sb("bn_x", [64, 6])
        mv_c = [sb(f"mv_c{i}", [P, 2]) for i in range(2)]
        mv_x = [sb(f"mv_x{i}", [64, 2]) for i in range(2)]
        var_sb = [sb(f"var_sb{i}", [P, 2]) for i in range(2)]
        rstd_sb = [sb(f"rstd_sb{i}", [P, 2]) for i in range(2)]
        power = sb("power", [P, 2])
        carry_pool = sb("carry_pool", [P, 2])
        carry_dve = sb("carry_dve", [P, 1])
        carry_act = sb("carry_act", [P, 1])
        ctx_n = sb("ctx_n", [P, D])
        x_n = sb("x_n", [64, D])
        ctx_t32 = sb("ctx_t32", [P, KT, P])
        x_t32 = sb("x_t32", [P, KT, 64])
        bn_h = sb("bn_h", [P, PER, 6])
        mv_h = sb("mv_h", [P, PER, 2])
        var_h = sb("var_h", [P, PER])
        rstd_h = sb("rstd_h", [P, PER])
        w_hi = [sb("w_hi0", [P, WC], F32R), sh.w_hi1]
        w_lo = [sb("w_lo0", [P, WC], F32R), sh.w_lo1]
        k_swap = sb("k_swap", [P, S])
        k_stack = [[sb(f"k_stack{i}{h}", [P, S], F32R) for h in range(2)] for i in range(2)]
        q_hi = sb("q_hi", [P, NQ], F32R)
        q_lo = sb("q_lo", [P, NQ], F32R)
        q_hh = [sb(f"q_hh{h}", [P, NQ], F32R) for h in range(2)]
        q_ll = [sb(f"q_ll{h}", [P, NQ], F32R) for h in range(2)]
        vT32 = sb("vT32", [P, S])
        v_hi = [sb(f"v_hi{i}", [P, S // P * 3 * DH], F32R) for i in range(2)]
        v_lo = [sb(f"v_lo{i}", [P, S // P * 3 * DH], F32R) for i in range(2)]
        probs = [sb(f"probs{i}", [P, 2, NQ]) for i in range(2)]
        p_hi = [sb(f"p_hi{i}", [P, 2, NQ], F32R) for i in range(2)]
        p_lo = [sb(f"p_lo{i}", [P, 2, NQ], F32R) for i in range(2)]

        score_ps = [psum(f"score_ps{i}", [P, 2, NQ]) for i in range(2)]
        o_ps = [psum(f"o_ps{h}", [P, NQ]) for h in range(2)]

        consts_loaded = sem("consts_loaded")
        ident_zero = sem("ident_zero")
        sin_signed = sem("sin_signed")
        y_zeroed = sem("y_zeroed")
        y_biased = sem("y_biased")
        ones_ready = sem("ones_ready")
        cols_loaded = sem("cols_loaded")
        rows_loaded = [sem(f"rows_loaded{i}") for i in range(2)]
        tile_loaded = [sem(f"tile_loaded{i}") for i in range(2)]
        bn_done = sem("bn_done")
        stats_ready = sem("stats_ready")
        aggregated = sem("aggregated")
        power_ready = sem("power_ready")
        rstd_ready = sem("rstd_ready")
        normed = sem("normed")
        turned = sem("turned")
        affine_done = sem("affine_done")
        tile_hi = sem("tile_hi")
        tile_split = sem("tile_split")
        w_loaded = sem("w_loaded")
        w_hi_done = sem("w_hi_done")
        k_projected = sem("k_projected")
        k_evac = sem("k_evac")
        k_swapped = sem("k_swapped")
        k_times = sem("k_times")
        k_roped = sem("k_roped")
        k_hi_done = sem("k_hi_done")
        k_split = sem("k_split")
        q_projected = sem("q_projected")
        q_hi_done = sem("q_hi_done")
        q_split = sem("q_split")
        q_stacked = [sem("q_stacked_a"), sem("q_stacked_b")]
        v_projected = sem("v_projected")
        v_evac = sem("v_evac")
        v_turned = sem("v_turned")
        v_hi_done = sem("v_hi_done")
        v_split = sem("v_split")
        scores_ready = sem("scores_ready")
        exp_done = sem("exp_done")
        clipped = sem("clipped")
        p_hi_done = sem("p_hi_done")
        p_split_dve = sem("p_split_dve")
        p_split_pool = sem("p_split_pool")
        pv_done = sem("pv_done")
        head_loaded = sem("head_loaded")
        sel_zero = sem("sel_zero")
        sel_hi_done = sem("sel_hi_done")
        sel_split = sem("sel_split")
        head_turned = sem("head_turned")
        head_added = sem("head_added")
        head_bn = sem("head_bn")
        head_aggregated = sem("head_aggregated")
        head_stats = sem("head_stats")
        head_rstd = sem("head_rstd")
        head_normed = sem("head_normed")
        head_x_turned = sem("head_x_turned")
        head_hi = sem("head_hi")
        head_split = sem("head_split")
        keys_loaded = sem("keys_loaded")
        key_hi_done = sem("key_hi_done")

        g_lat, b_lat, g_ctx, b_ctx, bo = (col_sb[:, 2 * i:2 * i + 2] for i in range(5))

        def v_part(v, tiles):
            at = slice(tiles.start * 3 * DH, tiles.stop * 3 * DH)
            return v[:, at].rearrange("p (t a d) -> p t a d", a=3, d=DH)[:, :, 0:3:2, :]

        def wait_split(eng, n, s):
            if s < 0:
                n, s = n - 1, s + STEPS
            if s in POOL_STEPS:
                wait(eng, p_split_pool, len(POOL_STEPS) * n + POOL_STEPS.index(s) + 1)
            else:
                wait(eng, p_split_dve, len(DVE_STEPS) * n + DVE_STEPS.index(s) + 1)

        def w_part(w, which, k):
            at = (which * KT + k) * P
            return w[:, at:at + P]

        x_nh = [ctx_n, ctx_raw[0], ctx_raw[1], ctx_t32]
        x_nh = [t[:].rearrange("p k n -> p (k n)") if t is ctx_t32 else t[:] for t in x_nh]

        rows_c = [p_[:].rearrange("p j (i d) -> p (j i) d", d=D) for p_ in probs]
        rows_x = [t[0:64, :].rearrange("p (i d) -> p i d", d=D) for t in (k_swap, vT32)]
        first_cn = [x2_head[:, i, :] for i in range(2)]
        first_xn = [den[0:64, i * D:(i + 1) * D] for i in range(2)]
        first_ct = [x2_head[:, 2 + i, :].rearrange("p (k n) -> p k n", k=KT) for i in range(2)]
        first_xt = [o_raw[:, i * P:(i + 1) * P].rearrange("p (k n) -> p k n", k=KT) for i in range(2)]

        key_raw = [k_swap, vT32, cos_sb, sin_sb]

        def lot_part(t, lot):
            return t[:, lot // 2, lot % 2, :]

        block = st.enter_context(nc.Block())

        @block.sync
        def _(sp):
            def load_tile(t):
                slot = t % 2 if isinstance(t, int) else t_slot[0]
                tt = t % (B * STEPS)
                sp.dma_start(ctx_raw[slot][:], ctx_in[bass.ds(tt * P, P), :]).then_inc(tile_loaded[slot], DMA)
                sp.dma_start(x_raw[slot][:], x[bass.ds(tt * 64, 64), :]).then_inc(tile_loaded[slot], DMA)

            t_slot = [0]

            def load_weights(w, has_wo=True):
                wait(sp, w_split, w)
                p = w % PAIRS
                for which, src, off in ((0, Wq, 0), (1, Wkv, 0), (2, Wkv, INNER)):
                    at = which * KT * P
                    sp.dma_start(
                        w_raw[:, at:at + KT * P].rearrange("c (k n) -> c k n", k=KT),
                        src[:, bass.ds(p * P + off, P)].rearrange("(k c) n -> c k n", k=KT),
                    ).then_inc(w_loaded, DMA)
                pw = (w + PAIRS - 2) % PAIRS
                sp.dma_start(w_raw[:, 3 * KT * P:], Wo[bass.ds(pw * P, P), :]).then_inc(w_loaded, DMA)

            def swap_k(p):
                wait(sp, k_evac, 2 * p + 2)
                wait(sp, k_roped, p)
                for q in range(4):
                    a, b = 32 * q, 32 * (q ^ 1)
                    sp.dma_start(k_swap[a:a + 32, :], k32[b:b + 32, :]).then_inc(k_swapped, DMA)

            def stack_q(p, h):
                wait(sp, scores_ready, STEPS * (p - 1) + 4 * (h + 1))
                src = slice(DH * h, DH * h + DH)
                for half in range(2):
                    dst = slice(DH * half, DH * half + DH)
                    sp.dma_start(raw(q_hh[h])[dst, :], raw(q_hi)[src, :]).then_inc(q_stacked[h], DMA)
                    sp.dma_start(raw(q_ll[h])[dst, :], raw(q_lo)[src, :]).then_inc(q_stacked[h], DMA)

            def load_rows(i):
                sp.dma_start(rows_c[i], ctx_in[512 * i:512 * (i + 1), :].rearrange("(t p) d -> p t d", p=P)
                             ).then_inc(rows_loaded[i], DMA)
                sp.dma_start(rows_x[i], x[256 * i:256 * (i + 1), :].rearrange("(t p) d -> p t d", p=64)
                             ).then_inc(rows_loaded[i], DMA)

            load_rows(0)
            sp.dma_start(col_sb[:], cols).then_inc(cols_loaded, DMA)
            load_weights(0)
            load_rows(1)
            for q in range(4):
                rows = slice(32 * q, 32 * q + 32)
                sp.dma_start(cos_sb[rows, :], cosT).then_inc(consts_loaded, DMA)
                sp.dma_start(sin_sb[rows, :], sinT).then_inc(consts_loaded, DMA)
            load_tile(8)
            load_tile(9)
            load_weights(1)
            swap_k(0)
            sp.wait_ge(q_split, 1)
            stack_q(0, 0)
            stack_q(0, 1)
            sp.wait_ge(normed, 2 * 9)
            load_tile(FIRST_TILES)
            load_weights(2)

            def iteration(n, par, project, prep):
                if project:
                    swap_k(n + 1)
                    wait(sp, q_split, n + 2)
                if prep:
                    t_slot[0] = 1 - par
                    load_tile(n + FIRST_TILES + 1)
                if project:
                    stack_q(n + 1, 0)
                    load_weights(n + 3)
                    stack_q(n + 1, 1)

            iteration(0, 0, True, True)
            iteration(1, 1, True, True)
            sp.wait_ge(tile_split, 2 * FIRST_TILES)
            sp.dma_start(x2_head[:], x[0:512, :].rearrange("(t p) d -> p t d", p=P)).then_inc(head_loaded, DMA)
            for k in range(KT):
                sp.dma_start(sh.sel_w[:, k, :], selT[k * P:(k + 1) * P, :]).then_inc(head_loaded, DMA)
            with sp.Fori(1, NPAIR // 2 - 1) as m:
                iteration(2 * m, 0, True, True)
                iteration(2 * m + 1, 1, True, True)
            iteration(NPAIR - 2, 0, True, False)
            sp.wait_ge(k_roped, NPAIR)
            sp.wait_ge(v_turned, 2 * NPAIR)
            for lot in range(4):
                k, e = lot // 2, 8 * (lot % 2)
                sp.dma_start(key_raw[lot][:].rearrange("p (e h) -> p e h", h=HID),
                             keys[e:e + 8, k * P:(k + 1) * P, :].rearrange("e d h -> d e h")).then_inc(keys_loaded, DMA)
            sp.wait_ge(w_split, NPAIR + 2)
            sp.dma_start(w_raw[:].rearrange("p (e d) -> p e d", d=D),
                         values[0:4, :, :].rearrange("e h d -> h e d")).then_inc(sh.first_values, DMA)
            store_gates(sp, sh, sel_dram, 0)
            sp.wait_ge(sh.gate_stored, DMA)
            sp.wait_ge(k_split, 2 * NPAIR)
            sp.dma_start(k32[:], sel_dram[0, 0:2, :].rearrange("e n -> (e n)").partition_broadcast(P)
                         ).then_inc(sh.first_gates, DMA)

        @block.gpsimd
        def _(pool):
            pool.memset(ident[:], 0.0).then_inc(ident_zero, 1)
            pool.wait_ge(ident_zero, 1)
            pool.affine_select(out=ident[:], in_=ident[:], compare_op=ALU.not_equal, fill=1.0, base=0,
                               pattern=[[-1, P]], channel_multiplier=1).then_inc(ident_ready, 1)

            def rstd(t, slot):
                wait(pool, stats_ready, 2 * t + 2)
                wait(pool, normed, 2 * (t - 1))
                pool.tensor_tensor(rstd_sb[slot][:], var_sb[slot][:], power[:], ALU.pow).then_inc(rstd_ready, 1)

            def split_first(t):
                pool.wait_ge(tile_hi, 2 * t + 2)
                bp, cs = t // STEPS, t % STEPS
                c_at, x_at = slice(cs * P, cs * P + P), slice(cs * 64, cs * 64 + 64)
                pool.tensor_tensor(ctxT_lo[:, bp, :, c_at], first_ct[t % 2], ctxT_hi[:, bp, :, c_at],
                                   ALU.subtract).then_inc(tile_split, 1)
                pool.tensor_tensor(xT_lo[:, bp, :, x_at], first_xt[t % 2], xT_hi[:, bp, :, x_at],
                                   ALU.subtract).then_inc(tile_split, 1)

            def split_tile(t):
                wait(pool, affine_done, 4 * t + 4)
                wait(pool, v_projected, 2 * (t - STEPS))
                bp = (t // STEPS) % 2
                cs = t % STEPS
                c_hi = ctxT_hi[:, bass.ds(bp, 1), :, bass.ds(cs * P, P)]
                c_lo = ctxT_lo[:, bass.ds(bp, 1), :, bass.ds(cs * P, P)]
                x_hi = xT_hi[:, bass.ds(bp, 1), :, bass.ds(cs * 64, 64)]
                x_lo = xT_lo[:, bass.ds(bp, 1), :, bass.ds(cs * 64, 64)]
                c32 = ctx_t32[:, :, :].rearrange("p (a k) n -> p a k n", a=1)
                x32 = x_t32[:, :, :].rearrange("p (a k) n -> p a k n", a=1)
                pool.tensor_copy(c_hi, c32).then_inc(tile_hi, 1)
                pool.tensor_copy(x_hi, x32).then_inc(tile_hi, 1)
                pool.wait_ge(tile_hi, 2 * t + 2)
                pool.tensor_tensor(c_lo, c32, c_hi, ALU.subtract).then_inc(tile_split, 1)
                pool.tensor_tensor(x_lo, x32, x_hi, ALU.subtract).then_inc(tile_split, 1)

            def round_weights(w, par):
                wait(pool, w_loaded, 4 * DMA * (w + 1))
                wait(pool, v_projected, 2 * (w - 1))
                wait(pool, y_projected, 2 * (w - 3))
                pool.tensor_tensor(carry_pool[:], power[:], power[:], ALU.add)
                pool.tensor_copy(w_hi[par][:, 0:WC // 2], w_raw[:, 0:WC // 2]).then_inc(w_hi_done, 1)

            def split_last(w, par):
                wait(pool, w_loaded, 4 * DMA * (w + 1))
                wait(pool, y_projected, 2 * (w - 3))
                pool.tensor_copy(w_hi[par][:, 3 * KT * P:], w_raw[:, 3 * KT * P:]).then_inc(w_hi_done, 2)
                pool.wait_ge(w_hi_done, 2 * (w + 1))
                pool.tensor_tensor(w_lo[par][:, 3 * KT * P:], w_raw[:, 3 * KT * P:], w_hi[par][:, 3 * KT * P:],
                                   ALU.subtract).then_inc(w_split, 1)

            def round_rest(w, par):
                pool.tensor_copy(w_hi[par][:, WC // 2:], w_raw[:, WC // 2:]).then_inc(w_hi_done, 1)

            def split_weights(w, par):
                pool.wait_ge(w_hi_done, 2 * (w + 1))
                pool.tensor_tensor(w_lo[par][:], w_raw[:], w_hi[par][:], ALU.subtract).then_inc(w_split, 1)

            def rope_times(p):
                wait(pool, k_swapped, 4 * DMA * (p + 1))
                pool.tensor_tensor(k_swap[:], k_swap[:], sin_sb[:], ALU.mult).then_inc(k_times, 1)

            for slot in range(2):
                pool.memset(var_sb[slot][:], 1.0).then_inc(power_ready, 1)
            pool.memset(power[:], -0.5).then_inc(power_ready, 1)
            pool.wait_ge(power_ready, 3)
            pool.memset(yT[:, :, :], 0.0).then_inc(y_zeroed, 1)
            for v, fill in ((v_hi, 1.0), (v_lo, 0.0)):
                for i in range(2):
                    middle = raw(v[i]).rearrange("p (t a d) -> p t a d", a=3, d=DH)[:, :, 1, :]
                    pool.memset(middle, fill).then_inc(ones_ready, 1)
            for t in range(STEPS):
                rstd(t, t % 2)
                if t >= 2:
                    split_first(t - 2)
            split_first(STEPS - 2)
            split_first(STEPS - 1)
            rstd(STEPS, 0)
            rstd(STEPS + 1, 1)
            pool.wait_ge(sin_signed, 2)
            rope_times(0)
            split_first(STEPS)
            split_first(STEPS + 1)

            def split_probs(n, s):
                wait(pool, p_hi_done, STEPS * n + s + 1)
                pool.tensor_tensor(p_lo[s % 2][:], probs[s % 2][:], p_hi[s % 2][:],
                                   ALU.subtract).then_inc(p_split_pool, 1)

            def iteration(n, par, project, prep):
                if prep:
                    rstd(n + FIRST_TILES, par)
                split_probs(n, 2)
                if project:
                    rope_times(n + 1)
                round_weights(n + 2, par)
                split_probs(n, 4)
                round_rest(n + 2, par)
                split_weights(n + 2, par)
                split_probs(n, 6)
                if prep:
                    split_tile(n + FIRST_TILES)

            iteration(0, 0, True, True)
            iteration(1, 1, True, True)
            with pool.Fori(1, NPAIR // 2 - 1) as m:
                iteration(2 * m, 0, True, True)
                iteration(2 * m + 1, 1, True, True)
            n = NPAIR - 2
            split_probs(n, 2)
            rope_times(n + 1)
            split_probs(n, 4)
            split_last(n + 2, 0)

            def head_norm(t):
                pool.wait_ge(head_stats, t + 2)
                pool.tensor_tensor(rstd_h[:, t:t + 2], var_h[:, t:t + 2], power[:], ALU.pow).then_inc(head_rstd, 1)
                pool.wait_ge(head_rstd, t // 2 + 1)
                pool.wait_ge(tile_loaded[0], 2 * DMA * ((NPAIR - 2 + FIRST_TILES) // 2 - 3))
                for i in (t, t + 1):
                    pool.tensor_scalar(x_nh[i], x2_head[:, i, :], mv_h[:, i, 0:1], rstd_h[:, i:i + 1],
                                       ALU.subtract, ALU.mult).then_inc(head_normed, 1)

            def split_keys(lot):
                pool.wait_ge(key_hi_done, lot + 1)
                pool.tensor_tensor(lot_part(ctxT_lo, lot), key_raw[lot][:], lot_part(ctxT_hi, lot),
                                   ALU.subtract).then_inc(sh.key_split, 1)

            head_norm(0)
            split_probs(n, 6)
            n = NPAIR - 1
            head_norm(2)
            split_probs(n, 2)
            split_last(n + 2, 1)
            split_probs(n, 4)
            split_keys(0)
            split_probs(n, 6)
            split_keys(2)

        @block.tensor
        def _(pe):
            def split_terms(par, which, rhs_hi, rhs_lo):
                terms = []
                for k in range(KT):
                    hi, lo = w_part(w_hi[par], which, k), w_part(w_lo[par], which, k)
                    terms += [(hi, rhs_hi(k)), (hi, rhs_lo(k)), (lo, rhs_hi(k))]
                return terms

            def ctx_cols(t, p, half):
                return lambda k: t[:, bass.ds((p // PAIRS) % 2, 1), k, bass.ds(half * 512, 512)]

            def x_cols(t, p):
                return lambda k: t[:, bass.ds((p // PAIRS) % 2, 1), k, :]

            def turn_tile(t):
                wait(pe, normed, 2 * t + 2)
                for k in range(KT):
                    pe.transpose(job_ps[1][:, k * P:(k + 1) * P], ctx_n[:, k * P:(k + 1) * P], ident[:])
                for k in range(KT):
                    tr = pe.transpose(job_ps[1][:, 256 + 64 * k:320 + 64 * k], x_n[:, k * P:(k + 1) * P],
                                      ident[0:64, 0:64])
                tr.then_inc(turned, 1)

            def project_k(p, par, half):
                if half == 0:
                    wait(pe, tile_split, 2 * (p + STEPS))
                    wait(pe, w_split, p + 1)
                wait(pe, y_added, 2 * (p - 2) - 1 + half)
                if isinstance(p, int) and p <= 2:
                    wait(pe, v_split, 2 * p - 1 + half)
                product(pe, job_ps[half][:], split_terms(par, 1, ctx_cols(ctxT_hi, p, half), ctx_cols(ctxT_lo, p, half))
                        ).then_inc(k_projected, 1)

            def project_q(p, par):
                wait(pe, k_evac, 2 * p + 1)
                product(pe, job_ps[0][:], split_terms(par, 0, x_cols(xT_hi, p), x_cols(xT_lo, p))
                        ).then_inc(q_projected, 1)

            def project_v(p, par, half):
                if half == 0:
                    wait(pe, q_split, p + 1)
                product(pe, job_ps[half][:], split_terms(par, 2, ctx_cols(ctxT_hi, p, half), ctx_cols(ctxT_lo, p, half))
                        ).then_inc(v_projected, 1)

            def turn_v(p, half):
                if half == 0:
                    wait(pe, v_evac, 2 * p + 2)
                for j in range(4):
                    tr = pe.transpose(job_ps[half][:, j * P:(j + 1) * P],
                                      vT32[:, (4 * half + j) * P:(4 * half + j + 1) * P], ident[:])
                tr.then_inc(v_turned, 1)

            def scores(n, s, par):
                g = STEPS * n + s
                h = s // 4
                if s % 4 == 0:
                    wait(pe, k_split, 2 * n + 1 + h)
                    wait(pe, q_stacked[h], 4 * DMA * (n + 1))
                wait(pe, exp_done, g - 1)
                for j in range(2):
                    tile = 2 * (s % 4) + j
                    keys = k_stack[par][h][:, tile * P:(tile + 1) * P]
                    mm = product(pe, score_ps[s % 2][:, j, :], [(keys, q_hh[h][:]), (keys, q_ll[h][:])])
                mm.then_inc(scores_ready, 1)

            def attend(n, s, par):
                g = STEPS * n + s
                h = s // 4
                if s == 0 and isinstance(n, int) and n <= 1:
                    wait(pe, v_split, 2 * n + 2)
                    wait(pe, ones_ready, 4)
                if s % 4 == 0:
                    wait(pe, o_evac[h], 2 * n)
                wait_split(pe, n, s)
                for j in range(2):
                    tile = 2 * (s % 4) + j
                    at = tile * 3 * DH + DH * h
                    hi, lo = v_hi[par][:, at:at + P], v_lo[par][:, at:at + P]
                    terms = [(hi, p_hi[s % 2][:, j, :]), (hi, p_lo[s % 2][:, j, :]), (lo, p_hi[s % 2][:, j, :])]
                    mm = product(pe, o_ps[h][:], terms, start=(tile == 0), stop=(tile == S // P - 1))
                mm.then_inc(pv_done, 1)

            pe.wait_ge(ident_ready, 1)
            def turn_first(t):
                wait(pe, normed, 2 * t + 2)
                wait(pe, tile_hi, 2 * (t - 1))
                bank = score_ps[0][:, t % 2, :]
                for k in range(KT):
                    pe.transpose(bank[:, k * P:(k + 1) * P], first_cn[t % 2][:, k * P:(k + 1) * P], ident[:])
                for k in range(KT):
                    tr = pe.transpose(bank[:, 256 + 64 * k:320 + 64 * k], first_xn[t % 2][:, k * P:(k + 1) * P],
                                      ident[0:64, 0:64])
                tr.then_inc(turned, 1)

            def first_product(which, half, done):
                if which == 0:
                    cols_ = lambda t: lambda k: t[:, 0, k, :]
                    terms = split_terms(0, 0, cols_(xT_hi), cols_(xT_lo))
                else:
                    cols_ = lambda t: lambda k: t[:, 0, k, half * 512:(half + 1) * 512]
                    terms = split_terms(0, which, cols_(ctxT_hi), cols_(ctxT_lo))
                product(pe, job_ps[half][:], terms).then_inc(done, 1)

            for t in range(STEPS):
                turn_first(t)
                if t == 6:
                    pe.wait_ge(tile_split, 2 * 4)
                    pe.wait_ge(w_split, 1)
                    first_product(1, 0, k_projected)
            pe.wait_ge(k_evac, 1)
            first_product(2, 0, v_projected)
            pe.wait_ge(tile_split, 2 * STEPS)
            first_product(1, 1, k_projected)
            pe.wait_ge(v_evac, 1)
            first_product(0, 0, q_projected)
            pe.wait_ge(k_evac, 2)
            first_product(2, 1, v_projected)
            turn_first(STEPS)
            turn_first(STEPS + 1)
            pe.wait_ge(q_split, 1)
            turn_v(0, 0)
            turn_v(0, 1)
            pe.wait_ge(tile_hi, 2 * FIRST_TILES)

            def head_turn_y(t):
                for i in range(2):
                    for mt in range(2):
                        tr = pe.transpose(job_ps[1][:, i * D + mt * P:i * D + (mt + 1) * P],
                                          yT[:, mt, (t + i) * P:(t + i + 1) * P], ident[:])
                tr.then_inc(head_turned, 1)

            def head_turn_x(t):
                pe.wait_ge(head_normed, t + 2)
                for k in range(KT):
                    for i in range(2):
                        tr = pe.transpose(job_ps[t // 2][:, (k * 2 + i) * P:(k * 2 + i + 1) * P],
                                          x_nh[t + i][:, k * P:(k + 1) * P], ident[:])
                tr.then_inc(head_x_turned, 1)

            def iteration(n, par, project, prep, first=False, head=False):
                nxt = 1 - par
                for s in range(STEPS):
                    scores(n, s, par)
                    if project:
                        if s < 2:
                            project_k(n + 1, nxt, s)
                        if s == 2:
                            project_q(n + 1, nxt)
                        if s == 3:
                            if prep:
                                wait(pe, k_evac, 2 * n + 4)
                                turn_tile(n + FIRST_TILES)
                            project_v(n + 1, nxt, 0)
                        if s == 4:
                            if head:
                                pe.wait_ge(head_added, 1)
                            if prep:
                                wait(pe, affine_done, 4 * (n + FIRST_TILES) + 4)
                            project_v(n + 1, nxt, 1)
                        if s in (5, 6):
                            turn_v(n + 1, s - 5)
                    if head:
                        if project and s == 3:
                            pe.wait_ge(k_evac, 2 * n + 4)
                            head_turn_y(0)
                        if not project and s == 0:
                            pe.wait_ge(y_added, 2 * (n - 1))
                            head_turn_y(2)
                        if not project and s == 1:
                            head_turn_x(0)
                        if not project and s == 3:
                            pe.wait_ge(head_added, 2)
                            head_turn_x(2)
                        if not project and s == 5:
                            pe.wait_ge(head_split, 2)
                            pe.wait_ge(sel_split, 1)
                            logits(pe, sh, lambda k: xT_hi[:, 0, k, :], lambda k: xT_lo[:, 0, k, :])
                    if s == 7 and not first:
                        if not project:
                            pe.wait_ge(sh.gate_exp, 1)
                        if project:
                            wait(pe, v_split, 2 * n + 3)
                        project_y(pe, sh, n - 1, 0, w_hi[nxt], w_lo[nxt])
                    if s >= LAG:
                        attend(n, s - LAG, par)
                    elif not first:
                        attend(n - 1, s - LAG + STEPS, nxt)
                    if s == 7 and not first:
                        if project:
                            wait(pe, v_split, 2 * n + 4)
                        project_y(pe, sh, n - 1, 1, w_hi[nxt], w_lo[nxt])

            iteration(0, 0, True, True, first=True)
            iteration(1, 1, True, True)
            with pe.Fori(1, NPAIR // 2 - 1) as m:
                iteration(2 * m, 0, True, True)
                iteration(2 * m + 1, 1, True, True)
            iteration(NPAIR - 2, 0, True, False, head=True)
            iteration(NPAIR - 1, 1, False, False, head=True)
            for s in range(STEPS - LAG, STEPS):
                attend(NPAIR - 1, s, 1)

        @block.scalar
        def _(act):
            def affine(t):
                wait(act, turned, t + 1)
                wait(act, tile_split, 2 * t)
                for k in range(KT):
                    act.activation(ctx_t32[:, k, :], job_ps[1][:, k * P:(k + 1) * P], ACT.Identity,
                                   bias=b_ctx[:, k:k + 1], scale=g_ctx[:, k:k + 1]).then_inc(affine_done, 1)
                for k in range(KT):
                    act.activation(x_t32[:, k, :], job_ps[1][:, 256 + 64 * k:320 + 64 * k], ACT.Identity,
                                   bias=b_lat[:, k:k + 1], scale=g_lat[:, k:k + 1]).then_inc(affine_done, 1)

            def evac_k(p, half):
                wait(act, k_projected, 2 * p + 1 + half)
                wait(act, k_split, 2 * p)
                act.copy(k32[:, half * 512:(half + 1) * 512], job_ps[half][:]).then_inc(k_evac, 1)

            def round_q(p):
                wait(act, q_projected, p + 1)
                for h in range(2):
                    wait(act, q_stacked[h], 4 * DMA * p)
                act.copy(q_hi[:], job_ps[0][:]).then_inc(q_hi_done, 1)

            def evac_v(p, half):
                wait(act, v_projected, 2 * p + 1 + half)
                wait(act, v_turned, 2 * p)
                act.copy(vT32[:, half * 512:(half + 1) * 512], job_ps[half][:]).then_inc(v_evac, 1)

            def round_v(p, par, half):
                wait(act, v_turned, 2 * p + 1 + half)
                wait(act, pv_done, STEPS * (p - 1))
                act.copy(v_part(v_hi[par], slice(4 * half, 4 * half + 4)),
                         job_ps[half][:].rearrange("p (t a d) -> p t a d", t=4, a=2)).then_inc(v_hi_done, 1)

            def round_k(p, par, h):
                wait(act, k_roped, p + 1)
                wait(act, scores_ready, STEPS * (p - 1))
                rows = slice(DH * h, DH * h + DH)
                act.copy(k_stack[par][h][rows, :], k32[rows, :]).then_inc(k_hi_done, 1)

            def exp(n, s):
                g = STEPS * n + s
                wait(act, scores_ready, g + 1)
                wait_split(act, n, s - 2)
                act.activation(probs[s % 2][:], score_ps[s % 2][:], ACT.Exp, scale=DH ** -0.5).then_inc(exp_done, 1)

            def round_probs(n, s):
                g = STEPS * n + s
                wait(act, clipped, g + 1)
                wait(act, pv_done, g - 1)
                act.copy(p_hi[s % 2][:], probs[s % 2][:]).then_inc(p_hi_done, 1)

            def evac_o(n, h):
                wait(act, pv_done, STEPS * n + 4 * h + 4)
                wait(act, o_split, n)
                dst = slice(DH * h, DH * h + DH)
                other = slice(DH * (1 - h), DH * (1 - h) + DH)
                act.copy(o_raw[dst, :], o_ps[h][dst, :]).then_inc(o_evac[h], 1)
                act.copy(den[dst, :], o_ps[h][other, :]).then_inc(o_evac[h], 1)

            def round_weights(w, par):
                act.wait_ge(w_loaded, 4 * DMA * (w + 1))
                act.copy(w_hi[par][:], w_raw[:]).then_inc(w_hi_done, 2)

            def affine_first(t):
                act.wait_ge(turned, t + 1)
                wait(act, tile_split, 2 * (t - 1))
                bank = score_ps[0][:, t % 2, :]
                bp, cs = t // STEPS, t % STEPS
                c_at, x_at = slice(cs * P, cs * P + P), slice(cs * 64, cs * 64 + 64)
                for c_to, x_to, done in ((first_ct[t % 2], first_xt[t % 2], None),
                                         (ctxT_hi[:, bp, :, c_at], xT_hi[:, bp, :, x_at], tile_hi)):
                    for k in range(KT):
                        a = act.activation(c_to[:, k, :], bank[:, k * P:(k + 1) * P], ACT.Identity,
                                           bias=b_ctx[:, k:k + 1], scale=g_ctx[:, k:k + 1])
                    a.then_inc(affine_done if done is None else done, 2 if done is None else 1)
                    for k in range(KT):
                        a = act.activation(x_to[:, k, :], bank[:, 256 + 64 * k:320 + 64 * k], ACT.Identity,
                                           bias=b_lat[:, k:k + 1], scale=g_lat[:, k:k + 1])
                    a.then_inc(affine_done if done is None else done, 2 if done is None else 1)

            act.wait_ge(power_ready, 3)
            act.activation(carry_act[:], power[:, 0:1], ACT.Exp)
            act.wait_ge(cols_loaded, DMA)
            for t in range(STEPS):
                affine_first(t)
                if t == 2:
                    round_weights(0, 0)
                if t == 6:
                    evac_k(0, 0)
            evac_v(0, 0)
            evac_k(0, 1)
            round_q(0)
            evac_v(0, 1)
            round_weights(1, 1)
            affine_first(STEPS)
            affine_first(STEPS + 1)
            round_v(0, 0, 0)
            round_v(0, 0, 1)
            round_k(0, 0, 0)
            round_k(0, 0, 1)

            def head_round(t):
                act.wait_ge(tile_split, 2 * (NPAIR - 2 + FIRST_TILES))
                act.wait_ge(head_x_turned, t // 2 + 1)
                act.copy(xT_hi[:, 0, :, t * P:(t + 2) * P],
                         job_ps[t // 2][:].rearrange("p (k n) -> p k n", k=KT)).then_inc(head_hi, 1)

            def round_keys(lot):
                act.wait_ge(tile_split, 2 * (NPAIR - 2 + FIRST_TILES))
                act.wait_ge(keys_loaded, 4 * DMA)
                act.copy(lot_part(ctxT_hi, lot), key_raw[lot][:]).then_inc(key_hi_done, 1)

            def iteration(n, par, project, prep, first=False, head=False):
                for s in range(STEPS):
                    exp(n, s)
                    if project:
                        if s < 2:
                            evac_k(n + 1, s)
                        if s == 2:
                            round_q(n + 1)
                        if s == 3:
                            if prep:
                                affine(n + FIRST_TILES)
                            evac_v(n + 1, 0)
                        if s == 4:
                            evac_v(n + 1, 1)
                        if s in (5, 6):
                            round_v(n + 1, 1 - par, s - 5)
                            round_k(n + 1, 1 - par, s - 5)
                    if s == 2 and not first:
                        evac_o(n - 1, 1)
                    if head:
                        if s in (1, 3):
                            head_round(s - 1)
                        if s == 5:
                            exp_gate(act, sh, 0)
                        if s >= 4:
                            round_keys(s - 4)
                    if s == 7:
                        evac_o(n, 0)
                    round_probs(n, s)

            iteration(0, 0, True, True, first=True)
            iteration(1, 1, True, True)
            with act.Fori(1, NPAIR // 2 - 1) as m:
                iteration(2 * m, 0, True, True)
                iteration(2 * m + 1, 1, True, True)
            iteration(NPAIR - 2, 0, True, False)
            iteration(NPAIR - 1, 1, False, False, head=True)
            evac_o(NPAIR - 1, 1)

        @block.vector
        def _(dve):
            def stats(t, slot):
                if isinstance(t, int) and t < STEPS:
                    dve.wait_ge(rows_loaded[t // 4], 2 * DMA)
                    c_rows, x_rows = rows_c[t // 4][:, t % 4, :], rows_x[t // 4][:, t % 4, :]
                else:
                    wait(dve, tile_loaded[slot], 2 * DMA * ((t - 6) // 2))
                    c_rows, x_rows = ctx_raw[slot][:], x_raw[slot][:]
                wait(dve, aggregated, 2 * t)
                dve.bn_stats(bn_c[:], c_rows).then_inc(bn_done, 1)
                dve.bn_stats(bn_x[:], x_rows).then_inc(bn_done, 1)
                dve.wait_ge(bn_done, 2 * t + 2)
                dve.tensor_copy(carry_dve[:], bn_c[:, 0:1])
                dve.bn_aggr(mv_c[slot][:], bn_c[:]).then_inc(aggregated, 1)
                dve.bn_aggr(mv_x[slot][:], bn_x[:]).then_inc(aggregated, 1)
                dve.wait_ge(aggregated, 2 * t + 2)
                dve.tensor_scalar(var_sb[slot][:, 0:1], mv_c[slot][:, 1:2], EPS, None, ALU.add).then_inc(stats_ready, 1)
                dve.tensor_scalar(var_sb[slot][0:64, 1:2], mv_x[slot][:, 1:2], 1.0 + EPS, EPS * EPS,
                                  ALU.mult, ALU.add).then_inc(stats_ready, 1)

            def normalize(t, slot):
                wait(dve, rstd_ready, t + 1)
                wait(dve, turned, t)
                dve.tensor_scalar(ctx_n[:], ctx_raw[slot][:], mv_c[slot][:, 0:1], rstd_sb[slot][:, 0:1],
                                  ALU.subtract, ALU.mult).then_inc(normed, 1)
                dve.tensor_scalar(x_n[:], x_raw[slot][:], mv_x[slot][:, 0:1], rstd_sb[slot][0:64, 1:2],
                                  ALU.subtract, ALU.mult).then_inc(normed, 1)

            def normalize_first(t):
                dve.wait_ge(rstd_ready, t + 1)
                wait(dve, turned, t - 1)
                slot = t % 2
                if t < STEPS:
                    c_rows, x_rows = rows_c[t // 4][:, t % 4, :], rows_x[t // 4][:, t % 4, :]
                else:
                    c_rows, x_rows = ctx_raw[slot][:], x_raw[slot][:]
                dve.tensor_scalar(first_cn[slot], c_rows, mv_c[slot][:, 0:1], rstd_sb[slot][:, 0:1],
                                  ALU.subtract, ALU.mult).then_inc(normed, 1)
                dve.tensor_scalar(first_xn[slot], x_rows, mv_x[slot][:, 0:1], rstd_sb[slot][0:64, 1:2],
                                  ALU.subtract, ALU.mult).then_inc(normed, 1)

            def split_weights(w, par):
                dve.wait_ge(w_hi_done, 2 * (w + 1))
                dve.tensor_tensor(w_lo[par][:], w_raw[:], w_hi[par][:], ALU.subtract).then_inc(w_split, 1)

            def split_q(p):
                wait(dve, q_hi_done, p + 1)
                for h in range(2):
                    wait(dve, q_stacked[h], 4 * DMA * p)
                dve.tensor_tensor(q_lo[:], job_ps[0][:], q_hi[:], ALU.subtract).then_inc(q_split, 1)

            def rope_times(p):
                wait(dve, k_evac, 2 * p + 2)
                wait(dve, k_swapped, 4 * DMA * (p + 1))
                dve.tensor_tensor(k32[:], k32[:], cos_sb[:], ALU.mult).then_inc(k_times, 1)

            def rope_add(p):
                wait(dve, k_times, 2 * p + 2)
                dve.tensor_tensor(k32[:], k32[:], k_swap[:], ALU.add).then_inc(k_roped, 1)

            def split_k(p, par, h):
                wait(dve, k_hi_done, 2 * p + 1 + h)
                rows = slice(DH * h, DH * h + DH)
                other = slice(DH * (1 - h), DH * (1 - h) + DH)
                dve.tensor_tensor(k_stack[par][h][other, :], k32[rows, :], k_stack[par][h][rows, :],
                                  ALU.subtract).then_inc(k_split, 1)

            def split_v(p, par, half):
                wait(dve, v_hi_done, 2 * p + 1 + half)
                tiles = slice(4 * half, 4 * half + 4)
                dve.tensor_tensor(v_part(v_lo[par], tiles), job_ps[half][:].rearrange("p (t a d) -> p t a d", t=4, a=2),
                                  v_part(v_hi[par], tiles), ALU.subtract).then_inc(v_split, 1)

            def split_probs(n, s):
                wait(dve, p_hi_done, STEPS * n + s + 1)
                dve.tensor_tensor(p_lo[s % 2][:], probs[s % 2][:], p_hi[s % 2][:],
                                  ALU.subtract).then_inc(p_split_dve, 1)

            def clip(n, s):
                g = STEPS * n + s
                wait(dve, exp_done, g + 1)
                dve.tensor_scalar(probs[s % 2][:], probs[s % 2][:], CLIP_HI, CLIP_LO,
                                  ALU.min, ALU.max).then_inc(clipped, 1)

            dve.wait_ge(power_ready, 3)
            stats(0, 0)
            for t in range(FIRST_TILES):
                if t + 1 < FIRST_TILES:
                    stats(t + 1, (t + 1) % 2)
                normalize_first(t)
                if t == 4:
                    split_weights(0, 0)
                if t == 7:
                    dve.wait_ge(y_zeroed, 1)
                    for mt in range(2):
                        dve.tensor_scalar(yT[:, mt, :], yT[:, mt, :], bo[:, mt:mt + 1], None,
                                          ALU.add).then_inc(y_biased, 1)
                    dve.wait_ge(y_biased, 2)
                if t == 6:
                    dve.wait_ge(consts_loaded, 8 * DMA)
                    for q in (0, 2):
                        rows = slice(32 * q, 32 * q + 32)
                        dve.tensor_scalar(sin_sb[rows, :], sin_sb[rows, :], -1.0, None, ALU.mult).then_inc(sin_signed, 1)
            split_q(0)
            split_weights(1, 1)
            rope_times(0)
            rope_add(0)
            split_k(0, 0, 0)
            split_k(0, 0, 1)
            split_v(0, 0, 0)
            split_v(0, 0, 1)

            dve.memset(raw(sh.sel_hi), 0.0).then_inc(sel_zero, 1)
            dve.memset(raw(sh.sel_lo), 0.0).then_inc(sel_zero, 1)

            def split_sel():
                dve.wait_ge(sel_zero, 2)
                dve.wait_ge(head_loaded, 3 * DMA)
                dve.tensor_copy(sh.sel_hi[:, :, 0:EXPERTS], sh.sel_w[:]).then_inc(sel_hi_done, 1)
                dve.wait_ge(sel_hi_done, 1)
                dve.tensor_tensor(sh.sel_lo[:, :, 0:EXPERTS], sh.sel_w[:], sh.sel_hi[:, :, 0:EXPERTS],
                                  ALU.subtract).then_inc(sel_split, 1)

            def head_rows(t):
                dve.wait_ge(head_loaded, 3 * DMA)
                dve.wait_ge(head_turned, t // 2 + 1)
                rows = x2_head[:, t:t + 2, :]
                dve.tensor_tensor(rows, job_ps[1][:].rearrange("p (i d) -> p i d", i=2), rows,
                                  ALU.add).then_inc(head_added, 1)
                dve.wait_ge(head_added, t // 2 + 1)
                for i in (t, t + 1):
                    dve.bn_stats(bn_h[:, i, :], x2_head[:, i, :]).then_inc(head_bn, 1)
                for i in (t, t + 1):
                    dve.wait_ge(head_bn, i + 1)
                    dve.bn_aggr(mv_h[:, i, :], bn_h[:, i, :]).then_inc(head_aggregated, 1)
                for i in (t, t + 1):
                    dve.wait_ge(head_aggregated, i + 1)
                    dve.tensor_scalar(var_h[:, i:i + 1], mv_h[:, i, 1:2], EPS, None, ALU.add).then_inc(head_stats, 1)

            def head_split_x(t):
                dve.wait_ge(head_hi, t // 2 + 1)
                at = slice(t * P, (t + 2) * P)
                dve.tensor_tensor(xT_lo[:, 0, :, at], job_ps[t // 2][:].rearrange("p (k n) -> p k n", k=KT),
                                  xT_hi[:, 0, :, at], ALU.subtract).then_inc(head_split, 1)

            def split_keys(lot):
                dve.wait_ge(key_hi_done, lot + 1)
                dve.tensor_tensor(lot_part(ctxT_lo, lot), key_raw[lot][:], lot_part(ctxT_hi, lot),
                                  ALU.subtract).then_inc(sh.key_split, 1)

            def iteration(n, par, project, prep, first=False, head=False):
                for s in range(STEPS):
                    clip(n, s)
                    if head:
                        if project and s == 1:
                            split_sel()
                        if project and s == 3:
                            head_rows(0)
                        if not project and s == 0:
                            head_rows(2)
                        if not project and s in (2, 4):
                            head_split_x(s - 2)
                    if s == 0 and prep:
                        stats(n + FIRST_TILES, par)
                    if s == 1 and prep:
                        normalize(n + FIRST_TILES, par)
                    if s == 2 and project:
                        split_q(n + 1)
                    if s in (2, 3) and not first:
                        invert_den(dve, sh, n - 1, s - 2)
                    if s == 4 and project:
                        rope_times(n + 1)
                    if s == 4 and project:
                        rope_add(n + 1)
                    if s == 5 and not first:
                        split_o(dve, sh, n - 1)
                    if s in (5, 6) and project:
                        split_v(n + 1, 1 - par, s - 5)
                    if s == 6 and project:
                        split_k(n + 1, 1 - par, 0)
                    if s >= 6 and head and not project:
                        invert_gate(dve, sh, 0, s - 6)
                    if s in (6, 7) and not first:
                        add_y(dve, sh, n - 1, s - 6)
                    if s in DVE_STEPS:
                        split_probs(n, s)
                    if s == 7 and project:
                        split_k(n + 1, 1 - par, 1)

            iteration(0, 0, True, True, first=True)
            iteration(1, 1, True, True)
            with dve.Fori(1, NPAIR // 2 - 1) as m:
                iteration(2 * m, 0, True, True)
                iteration(2 * m + 1, 1, True, True)
            iteration(NPAIR - 2, 0, True, False, head=True)
            iteration(NPAIR - 1, 1, False, False, head=True)
            split_keys(1)
            split_keys(3)


def ffn_phase(nc, sh, x, values, sel_dram, out):
    with ExitStack() as st:
        def sb(name, shape, dt=F32):
            return st.enter_context(nc.sbuf_tensor(name, shape, dt))

        def psum(name, shape):
            return st.enter_context(nc.psum_tensor(name, shape, F32))

        def sem(name):
            return st.enter_context(nc.semaphore(name))

        TILES = ALL // P
        ARING = 4
        FLAG = 3
        GROUP = 4
        FIRST_SHIFT = 2
        EVAC_AT, LOGITS_AT, TURN_OUT_AT, LAST_Y_AT = FLAG, 9, 12, 14

        yT, ident, turn_ps = sh.yT, sh.ident, sh.job_ps
        xT_hi, xT_lo, key_hi, key_lo = sh.xT_hi, sh.xT_lo, sh.wide_hi, sh.wide_lo
        logits_ready, gate_exp, gate_stored = sh.logits_ready, sh.gate_exp, sh.gate_stored

        x2 = sb("x2", [P, TILES, D])
        y_tile = sb("y_tile", [P, 2, 512])
        val_raw = sb("val_raw", [P, 8, D])
        val_hi = sb("val_hi", [P, EXPERTS, D], F32R)
        val_lo = sb("val_lo", [P, EXPERTS, D], F32R)
        bn = sb("bn2", [P, 6])
        mv = [sb(f"mv2{i}", [P, 2]) for i in range(2)]
        var_eps = [sb(f"var_eps{i}", [P, 1]) for i in range(2)]
        rstd = [sb(f"rstd2{i}", [P, 1]) for i in range(2)]
        power = sb("power2", [P, 1])
        carry = sb("carry2", [P, 2])
        spare = sb("spare", [P, 1])
        x_n = [sb(f"x_n2{i}", [P, D]) for i in range(2)]
        sel_all = [sb(f"sel_all{i}", [P, GROUP * 512]) for i in range(2)]
        act32 = [sb(f"act32{i}", [P, 512]) for i in range(ARING)]
        act_hi = [sb(f"act_hi{i}", [P, 512], F32R) for i in range(ARING)]
        act_lo = [sb(f"act_lo{i}", [P, 512], F32R) for i in range(ARING)]
        outT = sb("outT", [P, 2, 512])
        x_out = [sb(f"x_out{i}", [P, 2, D]) for i in range(2)]

        h_ps = [psum(f"h_ps{i}", [P, 512]) for i in range(ARING)]
        out_ps = [psum(f"out_ps{i}", [P, 512]) for i in range(2)]

        power_ready = sem("power_ready2")
        spare_set = sem("spare_set")
        x1_loaded = sem("x1_loaded")
        x_moved = sem("x_moved")
        y_copied = sem("y_copied")
        val_loaded = [sem(f"val_loaded{i}") for i in range(3)]
        val_hi_done = sem("val_hi_done")
        val_split = sem("val_split")
        y_turned = sem("y_turned")
        added = sem("added")
        bn_done = sem("bn_done2")
        aggregated = sem("aggregated2")
        stats_ready = sem("stats_ready2")
        rstd_ready = sem("rstd_ready2")
        normed = sem("normed2")
        x_turned = sem("x_turned")
        x_hi_done = sem("x_hi_done")
        x_split = sem("x_split")
        sel_loaded = [sem(f"sel_loaded{i}") for i in range(2)]
        h_ready = sem("h_ready")
        gated = sem("gated")
        act_hi_done = sem("act_hi_done")
        act_split = sem("act_split")
        summed = sem("summed")
        out_evac = sem("out_evac")
        out_turned = sem("out_turned")

        def added_before(c):
            return 0 if isinstance(c, int) and c == 0 else 6 * c - 2

        def lot_part(t, lot):
            return t[:, 4 * lot:4 * lot + 4, :]

        def values_of(lot):
            if lot in (0, 3):
                return sh.w_raw[:].rearrange("p (e d) -> p e d", d=D)
            return val_raw[:, 4 * lot - 4:4 * lot, :]

        block = st.enter_context(nc.Block())

        @block.sync
        def _(sp):
            def copy_y(c):
                wait(sp, y_turned, PER * (c - 1))
                sp.dma_start(y_tile[:], yT[:, :, bass.ds(c * 512, 512)]).then_inc(y_copied, DMA)

            def load_gates(c, q, slot):
                wait(sp, gated, GROUP * (EXPERTS // GROUP * c + q - 1))
                src = sel_dram[bass.ds(c, 1), GROUP * q:GROUP * q + GROUP, :].rearrange("a e n -> a (e n)")
                sp.dma_start(sel_all[slot][:], src[0, :].partition_broadcast(P)).then_inc(sel_loaded[slot], DMA)

            def store(c, first_sum):
                for i in range(2):
                    wait(sp, added, first_sum + i)
                    sp.dma_start(out[bass.ds(c * 512 + i * 256, 256), :].rearrange("(t p) d -> p t d", p=P),
                                 x_out[i][:]).then_inc(x_moved, DMA)

            load_gates(0, 0, 0)
            sp.dma_start(y_tile[:], yT[:, :, 512:1024]).then_inc(y_copied, DMA)
            sp.dma_start(x2[:, PER:2 * PER, :],
                         x[512:1024, :].rearrange("(t p) d -> p t d", p=P)).then_inc(x1_loaded, DMA)
            load_gates(0, 1, 1)
            for lot in range(1, 4):
                if lot == 3:
                    sp.wait_ge(val_split, 1)
                sp.dma_start(values_of(lot),
                             values[4 * lot:4 * lot + 4, :, :].rearrange("e h d -> h e d")
                             ).then_inc(val_loaded[lot - 1], DMA)
            sp.dma_start(x2[:, 0:PER, :], sh.x2_head[:]).then_inc(x_moved, DMA)
            for q in range(2, CHUNKS):
                sp.dma_start(x2[:, PER * q:PER * (q + 1), :],
                             x[512 * q:512 * (q + 1), :].rearrange("(t p) d -> p t d", p=P)).then_inc(x_moved, DMA)

            def chunk(c, first=False, last=False, copy=True):
                load_gates(c, 2, 0)
                load_gates(c, 3, 1)
                if not last:
                    if copy:
                        copy_y(c + 2)
                    store_gates(sp, sh, sel_dram, c + 1)
                    wait(sp, gate_stored, DMA * (c + 2))
                    load_gates(c + 1, 0, 0)
                if not first:
                    store(c - 1, added_before(c) + 1 + (0 if last else PER))
                if not last:
                    load_gates(c + 1, 1, 1)

            chunk(0, first=True)
            sp.wait_ge(sh.y_added, 2 * NPAIR)
            with sp.Fori(1, CHUNKS - 2) as c:
                chunk(c)
            chunk(CHUNKS - 2, copy=False)
            chunk(CHUNKS - 1, last=True)
            store(CHUNKS - 1, added_before(CHUNKS - 1) + 3)
            sp.wait_ge(x_moved, DMA * (3 + 2 * CHUNKS))

        @block.gpsimd
        def _(pool):
            pool.memset(power[:], -0.5).then_inc(power_ready, 1)
            pool.wait_ge(power_ready, 1)

            def invert_std(t, slot):
                wait(pool, stats_ready, t + 1)
                wait(pool, normed, t - 1)
                pool.tensor_tensor(rstd[slot][:], var_eps[slot][:], power[:], ALU.pow).then_inc(rstd_ready, 1)

            def split_values(lot):
                pool.wait_ge(val_hi_done, lot + 1)
                pool.tensor_tensor(lot_part(val_lo, lot), values_of(lot), lot_part(val_hi, lot),
                                   ALU.subtract).then_inc(val_split, 1)

            def split_act(g, e):
                wait(pool, act_hi_done, g + 1)
                pool.tensor_tensor(act_lo[e % ARING][:], act32[e % ARING][:], act_hi[e % ARING][:],
                                   ALU.subtract).then_inc(act_split, 1)

            def chunk(c, first=False, last=False):
                for e in range(EXPERTS):
                    split_act(EXPERTS * c + e, e)
                    a = e - (FIRST_SHIFT if first else 0)
                    if not last and a % 2 == 0 and 0 <= a < 2 * PER:
                        invert_std(PER * c + a // 2, a // 2 % 2)
                    if first and e % 3 == 0 and e < 12:
                        split_values(e // 3)

            chunk(0, first=True)
            with pool.Fori(1, CHUNKS - 1) as c:
                chunk(c)
            chunk(CHUNKS - 1, last=True)

        @block.tensor
        def _(pe):
            def turn_y(src, at):
                for mt in range(2):
                    tr = pe.transpose(turn_ps[0][:, mt * P:(mt + 1) * P], src[:, mt, at:at + P], ident[:])
                tr.then_inc(y_turned, 1)

            def turn_x(t, slot):
                wait(pe, normed, t + 1)
                wait(pe, x_split, t)
                for k in range(KT):
                    tr = pe.transpose(turn_ps[1][:, k * P:(k + 1) * P], x_n[slot][:, k * P:(k + 1) * P], ident[:])
                tr.then_inc(x_turned, 1)

            def chunk_cols(t, c):
                return lambda k: t[:, bass.ds(c % 2, 1), k, :]

            def chunk_logits(c):
                wait(pe, x_split, PER * c)
                logits(pe, sh, chunk_cols(xT_hi, c), chunk_cols(xT_lo, c))

            pe.wait_ge(sh.key_split, 4)

            def expert_in(c, g, e):
                wait(pe, gated, g - ARING + 1)
                x_hi, x_lo = chunk_cols(xT_hi, c), chunk_cols(xT_lo, c)
                at = slice(e % 8 * HID, (e % 8 + 1) * HID)
                terms = []
                for k in range(KT):
                    hi, lo = key_hi[:, k, e // 8, at], key_lo[:, k, e // 8, at]
                    terms += [(hi, x_hi(k)), (hi, x_lo(k)), (lo, x_hi(k))]
                product(pe, h_ps[e % ARING][:], terms).then_inc(h_ready, 1)

            def expert_out(c, g, e):
                wait(pe, act_split, g + 1)
                for mt in range(2):
                    if e == 0:
                        wait(pe, out_evac, 2 * (c - 1) + 1 + mt)
                    hi, lo = val_hi[:, e, mt * P:(mt + 1) * P], val_lo[:, e, mt * P:(mt + 1) * P]
                    mm = product(pe, out_ps[mt][:], [(hi, act_hi[e % ARING][:]), (hi, act_lo[e % ARING][:]),
                                                     (lo, act_hi[e % ARING][:])],
                                 start=(e == 0), stop=(e == EXPERTS - 1))
                mm.then_inc(summed, 1)

            def turn_out(c):
                wait(pe, out_evac, 2 * c + 2)
                for i in range(2):
                    for j in range(2):
                        for mt in range(2):
                            at = (2 * i + j) * P
                            tr = pe.transpose(turn_ps[1 - i][:, j * D + mt * P:j * D + (mt + 1) * P],
                                              outT[:, mt, at:at + P], ident[:])
                    tr.then_inc(out_turned, 1)

            def chunk(c, first=False, last=False):
                for e in range(EXPERTS):
                    g = EXPERTS * c + e
                    expert_in(c, g, e)
                    a = e - (FIRST_SHIFT if first else 0)
                    if not last:
                        if a % 2 == 0 and 0 < a <= 2 * PER:
                            turn_x(PER * c + a // 2 - 1, (a // 2 - 1) % 2)
                        if a % 2 == 0 and 0 <= a < 2 * PER:
                            if a == 0:
                                wait(pe, y_copied, DMA * (c + 1))
                                wait(pe, gate_exp, c + 1)
                            wait(pe, added, added_before(c) + a // 2)
                            turn_y(y_tile, a // 2 * P)
                        if a == LOGITS_AT:
                            wait(pe, added, added_before(c) + PER)
                            chunk_logits(c + 1)
                    if e == TURN_OUT_AT and not first:
                        if last:
                            wait(pe, added, added_before(c))
                        else:
                            wait(pe, gate_exp, c + 2)
                            wait(pe, x_split, PER * (c + 1))
                        turn_out(c - 1)
                    if first and e == LAST_Y_AT:
                        pe.wait_ge(gate_exp, 2)
                        pe.wait_ge(x_split, PER)
                        for mt in range(2):
                            project_y(pe, sh, NPAIR - 1, mt, sh.w_hi1, sh.w_lo1)
                    if first and e >= FLAG and (e - FLAG) % 4 == 0:
                        pe.wait_ge(val_split, (e - FLAG) // 4 + 1)
                    if e >= FLAG:
                        expert_out(c, g - FLAG, e - FLAG)
                    elif not first:
                        expert_out(c - 1, g - FLAG, e - FLAG + EXPERTS)

            chunk(0, first=True)
            pe.wait_ge(sh.y_added, 2 * NPAIR)
            with pe.Fori(1, CHUNKS - 1) as c:
                chunk(c)
            chunk(CHUNKS - 1, last=True)
            for e in range(EXPERTS - FLAG, EXPERTS):
                expert_out(CHUNKS - 1, EXPERTS * (CHUNKS - 1) + e, e)
            pe.wait_ge(added, added_before(CHUNKS - 1) + 2)
            turn_out(CHUNKS - 1)

        @block.scalar
        def _(act):
            def round_x(t, c, j):
                wait(act, x_turned, t + 1)
                act.copy(xT_hi[:, bass.ds(c % 2, 1), :, j * P:(j + 1) * P],
                         turn_ps[1][:, 0:KT * P].rearrange("p (a k n) -> p a k n", a=1, k=KT)).then_inc(x_hi_done, 1)

            def round_values(lot):
                act.wait_ge(sh.first_values if lot == 0 else val_loaded[lot - 1], DMA)
                act.copy(lot_part(val_hi, lot), values_of(lot)).then_inc(val_hi_done, 1)

            def round_act(g, e):
                wait(act, gated, g + 1)
                wait(act, summed, g - ARING + 1)
                act.copy(act_hi[e % ARING][:], act32[e % ARING][:]).then_inc(act_hi_done, 1)

            def evac_out(c):
                wait(act, summed, EXPERTS * (c + 1))
                for mt in range(2):
                    act.copy(outT[:, mt, :], out_ps[mt][:]).then_inc(out_evac, 1)

            def chunk(c, first=False, last=False):
                for e in range(EXPERTS):
                    if e == EVAC_AT and not first:
                        evac_out(c - 1)
                    if first and e % 3 == 0 and e < 12:
                        round_values(e // 3)
                    a = e - (FIRST_SHIFT if first else 0)
                    round_act(EXPERTS * c + e, e)
                    if not last:
                        if a % 2 == 0 and 0 < a <= 2 * PER:
                            round_x(PER * c + a // 2 - 1, c + 1, a // 2 - 1)
                        if a == LOGITS_AT:
                            exp_gate(act, sh, c + 1)

            chunk(0, first=True)
            with act.Fori(1, CHUNKS - 1) as c:
                chunk(c)
            chunk(CHUNKS - 1, last=True)
            evac_out(CHUNKS - 1)

        @block.vector
        def _(dve):
            def residual(t, slot):
                wait(dve, y_turned, t + 1)
                row = x2[:, bass.ds(t + PER, 1), :].rearrange("p a d -> p (a d)")
                dve.tensor_tensor(row, turn_ps[0][:, 0:D], row, ALU.add).then_inc(added, 1)

            def stats(t, slot, count):
                wait(dve, added, count)
                wait(dve, aggregated, t)
                dve.tensor_copy(carry[:, 0:1], spare[:])
                row = x2[:, bass.ds(t + PER, 1), :].rearrange("p a d -> p (a d)")
                dve.bn_stats(bn[:], row).then_inc(bn_done, 1)
                wait(dve, bn_done, t + 1)
                dve.tensor_copy(carry[:, 1:2], bn[:, 0:1])
                dve.bn_aggr(mv[slot][:], bn[:]).then_inc(aggregated, 1)
                wait(dve, aggregated, t + 1)
                dve.tensor_scalar(var_eps[slot][:], mv[slot][:, 1:2], EPS, None, ALU.add).then_inc(stats_ready, 1)

            def normalize(t, slot):
                wait(dve, rstd_ready, t + 1)
                wait(dve, x_turned, t - 1)
                row = x2[:, bass.ds(t + PER, 1), :].rearrange("p a d -> p (a d)")
                dve.tensor_scalar(x_n[slot][:], row, mv[slot][:, 0:1], rstd[slot][:],
                                  ALU.subtract, ALU.mult).then_inc(normed, 1)

            def split_x(t, c, j):
                wait(dve, x_hi_done, t + 1)
                at = slice(j * P, (j + 1) * P)
                dve.tensor_tensor(xT_lo[:, bass.ds(c % 2, 1), :, at],
                                  turn_ps[1][:, 0:KT * P].rearrange("p (a k n) -> p a k n", a=1, k=KT),
                                  xT_hi[:, bass.ds(c % 2, 1), :, at], ALU.subtract).then_inc(x_split, 1)

            dve.memset(spare[:], 0.0).then_inc(spare_set, 1)
            dve.wait_ge(spare_set, 1)

            def gate_h(c, e):
                g = EXPERTS * c + e
                wait(dve, h_ready, g + 1)
                q = e // GROUP
                first_two = isinstance(c, int) and c == 0 and e < 2
                if first_two:
                    dve.wait_ge(sh.first_gates, DMA)
                elif e % GROUP == 0 or (e == 2 and isinstance(c, int) and c == 0):
                    wait(dve, sel_loaded[q % 2], DMA * (2 * c + q // 2 + 1))
                wait(dve, act_split, g - ARING + 1)
                at = (e % GROUP) * 512
                gates = sh.k32 if first_two else sel_all[q % 2]
                dve.scalar_tensor_tensor(out=act32[e % ARING][:], in0=h_ps[e % ARING][:], scalar=0.0,
                                         in1=gates[:, at:at + 512], op0=ALU.max, op1=ALU.mult
                                         ).then_inc(gated, 1)

            def add_out(c, i):
                wait(dve, out_turned, 2 * c + i + 1)
                wait(dve, x_moved, DMA * (3 + 2 * c))
                dve.tensor_tensor(x_out[i][:], turn_ps[1 - i][:].rearrange("p (t d) -> p t d", d=D),
                                  x2[:, bass.ds(c * PER + 2 * i, 2), :], ALU.add).then_inc(added, 1)

            def chunk(c, first=False, last=False):
                for e in range(EXPERTS):
                    gate_h(c, e)
                    a = e - (FIRST_SHIFT if first else 0)
                    t, j = PER * c + a // 2, a // 2
                    if a == 0 and not last:
                        if first:
                            dve.wait_ge(x1_loaded, DMA)
                        else:
                            dve.wait_ge(x_moved, 3 * DMA)
                    if not last:
                        if a % 2 == 0 and 0 <= a < 2 * PER:
                            residual(t, j % 2)
                            stats(t, j % 2, added_before(c) + j + 1)
                        if a % 2 == 1 and 0 <= a < 2 * PER:
                            normalize(t, j % 2)
                        if a % 2 == 0 and 0 < a <= 2 * PER:
                            split_x(t - 1, c + 1, j - 1)
                        if a in (LOGITS_AT + 1, LOGITS_AT + 2):
                            invert_gate(dve, sh, c + 1, a - LOGITS_AT - 1)
                    if first and e in (4, 6):
                        invert_den(dve, sh, NPAIR - 1, e // 2 - 2)
                    if first and e == 8:
                        split_o(dve, sh, NPAIR - 1)
                    if first and e == LAST_Y_AT:
                        add_y(dve, sh, NPAIR - 1, 0)
                        add_y(dve, sh, NPAIR - 1, 1)
                    if e in (TURN_OUT_AT, TURN_OUT_AT + 1) and not first:
                        add_out(c - 1, e - TURN_OUT_AT)

            chunk(0, first=True)
            with dve.Fori(1, CHUNKS - 1) as c:
                chunk(c)
            chunk(CHUNKS - 1, last=True)
            for i in range(2):
                add_out(CHUNKS - 1, i)


def build(nc, x, ctx_in, cosT, sinT, cols, Wq, Wkv, Wo, selT, keys, values, out, sel_dram):
    with ExitStack() as st:
        sh = shared_state(nc, st)
        attention_phase(nc, sh, x, ctx_in, cosT, sinT, cols, Wq, Wkv, Wo, selT, keys, values, sel_dram)
        ffn_phase(nc, sh, x, values, sel_dram, out)


def kernel(x, ctx_1024, L0_xattn_cos, L0_xattn_sin, L0_xattn_ln_lat_g, L0_xattn_ln_lat_b, L0_xattn_ln_ctx_g,
           L0_xattn_ln_ctx_b, L0_xattn_Wq, L0_xattn_Wkv, L0_xattn_Wo, L0_xattn_bo, L0_ffn_expert_sel,
           L0_ffn_keys, L0_ffn_values):
    import numpy as np
    import concourse.bacc as bacc
    from concourse.bass_utils import run_bass_kernel_spmd

    vectors = [L0_xattn_ln_lat_g, L0_xattn_ln_lat_b, L0_xattn_ln_ctx_g, L0_xattn_ln_ctx_b, L0_xattn_bo]
    cols = np.concatenate([np.asarray(v).reshape(KT, P) for v in vectors], axis=0).T
    arrays = {
        "x": np.asarray(x).reshape(ALL, D),
        "ctx": np.asarray(ctx_1024).reshape(B * S, D),
        "cosT": np.asarray(L0_xattn_cos).T,
        "sinT": np.asarray(L0_xattn_sin).T,
        "cols": cols,
        "Wq": L0_xattn_Wq,
        "Wkv": L0_xattn_Wkv,
        "Wo": L0_xattn_Wo,
        "selT": np.asarray(L0_ffn_expert_sel).T,
        "keys": L0_ffn_keys,
        "values": L0_ffn_values,
    }
    arrays = {name: np.ascontiguousarray(a) for name, a in arrays.items()}
    nc = bacc.Bacc("TRN2", target_bir_lowering=False, num_devices=1)
    ins = [nc.dram_tensor(name, a.shape, mybir.dt.from_np(a.dtype), kind="ExternalInput").ap()
           for name, a in arrays.items()]
    out = nc.dram_tensor("out", (ALL, D), F32, kind="ExternalOutput").ap()
    sel_dram = nc.dram_tensor("sel_dram", (CHUNKS, EXPERTS, 512), F32, kind="Internal").ap()
    build(nc, *ins, out, sel_dram)
    r = run_bass_kernel_spmd(nc, [arrays], core_ids=[0])
    return r.results[0]["out"].reshape(B, NQ, D)
```
